# Optimizing a Trainium2 kernel written in Bass

```python
import numpy as np
import jax
import jax.numpy as jnp

def _softmax(x, axis=-1):
    return jax.nn.softmax(x, axis=axis)

def _gelu(x):
    return jax.nn.gelu(x, approximate=True)

def _silu(x):
    return jax.nn.silu(x)

def _sigmoid(x):
    return jax.nn.sigmoid(x)

def _layernorm(x, axis=-1, eps=1e-05):
    m = jnp.mean(x, axis=axis, keepdims=True)
    v = jnp.var(x, axis=axis, keepdims=True)
    return (x - m) / jnp.sqrt(v + eps)

def _scatter_add(tgt, idx, src, axis=0):
    return tgt.at[idx].add(src)

def _segment_sum(src, seg, n):
    return jax.ops.segment_sum(src, seg, n)
kernel_name = 'mk_sandwich_d1_jaxref_r8_02bf34'

def setup_inputs(seed: int=0):
    np.random.seed(seed)
    _w = jnp.asarray

    def _L0_attn_setup():
        import jax, jax.numpy as jnp
        import numpy as np
        B_SZ, L, D_MODEL = (2, 128, 128)
        D_INNER, D_STATE, D_CONV = (256, 16, 4)
        EPS = 1e-06

        def _selective_scan(xc, delta, A, Bm, Cm, D_skip):
            dA = jnp.exp(delta[..., None] * A)
            dBx = (delta * xc)[..., None] * Bm[:, :, None, :]
            h0 = jnp.zeros((xc.shape[0], xc.shape[2], A.shape[1]), xc.dtype)

            def step(h, inp):
                dA_t, dBx_t, C_t = inp
                h = dA_t * h + dBx_t
                y_t = jnp.einsum('bds,bs->bd', h, C_t)
                return (h, y_t)
            _, ys = jax.lax.scan(step, h0, (dA.transpose(1, 0, 2, 3), dBx.transpose(1, 0, 2, 3), Cm.transpose(1, 0, 2)))
            y = ys.transpose(1, 0, 2)
            return y + D_skip * xc

        def _layernorm(r, alpha, beta):
            mean = jnp.mean(r, axis=-1, keepdims=True)
            diff = r - mean
            var_unb = jnp.sum(diff * diff, axis=-1, keepdims=True) / (r.shape[-1] - 1)
            std = jnp.sqrt(var_unb)
            return alpha * diff / (std + EPS) + beta
        key = jax.random.key(seed)
        ks = jax.random.split(key, 8)

        def n(k, shape, scale=0.02):
            return jax.random.normal(k, shape, jnp.float32) * scale
        return {'x': jax.random.normal(ks[0], (B_SZ, L, D_MODEL), jnp.float32), 'W_in': n(ks[1], (D_MODEL, 2 * D_INNER)), 'b_in': jnp.zeros((2 * D_INNER,), jnp.float32), 'conv_w': n(ks[2], (D_INNER, 1, D_CONV), 0.2), 'conv_b': jnp.zeros((D_INNER,), jnp.float32), 'W_xp': n(ks[3], (D_INNER, 2 * D_STATE)), 'b_xp': jnp.zeros((2 * D_STATE,), jnp.float32), 'W_dt': n(ks[4], (D_INNER, D_INNER)), 'b_dt': jnp.full((D_INNER,), -1.0, jnp.float32), 'A_log': jnp.log(jax.random.uniform(ks[5], (D_INNER, D_STATE), jnp.float32, 0.5, 1.5)), 'D_skip': jnp.ones((D_INNER,), jnp.float32), 'W_out': n(ks[6], (D_INNER, D_MODEL)), 'b_out': jnp.zeros((D_MODEL,), jnp.float32), 'alpha': jnp.ones((D_MODEL,), jnp.float32), 'beta': jnp.zeros((D_MODEL,), jnp.float32)}
    _L0_attn_in = _L0_attn_setup()

    def _L0_ffn_setup():
        import jax, jax.numpy as jnp
        import numpy as np
        FP8_E4M3_MAX = 448.0

        def fake_quant_fp8(t):
            amax = jnp.max(jnp.abs(t))
            scale = FP8_E4M3_MAX / jnp.maximum(amax, 1e-12)
            q = (t * scale).astype(jnp.float8_e4m3fn).astype(jnp.float32)
            return q / scale
        key = jax.random.key(seed)
        k1, k2, k3 = jax.random.split(key, 3)
        d_in, d_out = (128, 128)
        x = jax.random.normal(k1, (4, 1024, d_in), dtype=jnp.float32)
        weight = jax.random.normal(k2, (d_out, d_in), dtype=jnp.float32) * (1.0 / np.sqrt(d_in))
        bias = jax.random.normal(k3, (d_out,), dtype=jnp.float32) * 0.01
        return {'x': x, 'weight': weight, 'bias': bias}
    _L0_ffn_in = _L0_ffn_setup()
    _d = {'L0_attn_x': _L0_attn_in['x'], 'L0_attn_W_in': _L0_attn_in['W_in'], 'L0_attn_b_in': _L0_attn_in['b_in'], 'L0_attn_conv_w': _L0_attn_in['conv_w'], 'L0_attn_conv_b': _L0_attn_in['conv_b'], 'L0_attn_W_xp': _L0_attn_in['W_xp'], 'L0_attn_b_xp': _L0_attn_in['b_xp'], 'L0_attn_W_dt': _L0_attn_in['W_dt'], 'L0_attn_b_dt': _L0_attn_in['b_dt'], 'L0_attn_A_log': _L0_attn_in['A_log'], 'L0_attn_D_skip': _L0_attn_in['D_skip'], 'L0_attn_W_out': _L0_attn_in['W_out'], 'L0_attn_b_out': _L0_attn_in['b_out'], 'L0_attn_alpha': _L0_attn_in['alpha'], 'L0_attn_beta': _L0_attn_in['beta'], 'L0_ffn_weight': _L0_ffn_in['weight'], 'L0_ffn_bias': _L0_ffn_in['bias']}
    _x0 = _d['L0_attn_x']
    _d['L0_attn_x'] = jax.random.normal(jax.random.fold_in(jax.random.key(seed), 1), (16, 256, 128), dtype=_x0.dtype)
    del _x0
    return _d

def reference(L0_attn_x, L0_attn_W_in, L0_attn_b_in, L0_attn_conv_w, L0_attn_conv_b, L0_attn_W_xp, L0_attn_b_xp, L0_attn_W_dt, L0_attn_b_dt, L0_attn_A_log, L0_attn_D_skip, L0_attn_W_out, L0_attn_b_out, L0_attn_alpha, L0_attn_beta, L0_ffn_weight, L0_ffn_bias):

    def _L0_attn_ref(x, W_in, b_in, conv_w, conv_b, W_xp, b_xp, W_dt, b_dt, A_log, D_skip, W_out, b_out, alpha, beta):
        import jax, jax.numpy as jnp
        import numpy as np
        B_SZ, L, D_MODEL = (2, 128, 128)
        D_INNER, D_STATE, D_CONV = (256, 16, 4)
        EPS = 1e-06

        def _selective_scan(xc, delta, A, Bm, Cm, D_skip):
            dA = jnp.exp(delta[..., None] * A)
            dBx = (delta * xc)[..., None] * Bm[:, :, None, :]
            h0 = jnp.zeros((xc.shape[0], xc.shape[2], A.shape[1]), xc.dtype)

            def step(h, inp):
                dA_t, dBx_t, C_t = inp
                h = dA_t * h + dBx_t
                y_t = jnp.einsum('bds,bs->bd', h, C_t)
                return (h, y_t)
            _, ys = jax.lax.scan(step, h0, (dA.transpose(1, 0, 2, 3), dBx.transpose(1, 0, 2, 3), Cm.transpose(1, 0, 2)))
            y = ys.transpose(1, 0, 2)
            return y + D_skip * xc

        def _layernorm(r, alpha, beta):
            mean = jnp.mean(r, axis=-1, keepdims=True)
            diff = r - mean
            var_unb = jnp.sum(diff * diff, axis=-1, keepdims=True) / (r.shape[-1] - 1)
            std = jnp.sqrt(var_unb)
            return alpha * diff / (std + EPS) + beta
        residual = x
        xz = x @ W_in + b_in
        x_in, z = jnp.split(xz, 2, axis=-1)
        xt = x_in.transpose(0, 2, 1)
        xt = jax.lax.conv_general_dilated(xt, conv_w, window_strides=(1,), padding=[(D_CONV - 1, 0)], feature_group_count=D_INNER, dimension_numbers=('NCH', 'OIH', 'NCH'))
        xt = xt + conv_b[None, :, None]
        x_conv = jax.nn.silu(xt.transpose(0, 2, 1))
        x_proj_out = x_conv @ W_xp + b_xp
        Bm, Cm = jnp.split(x_proj_out, 2, axis=-1)
        delta = jax.nn.softplus(x_conv @ W_dt + b_dt)
        A = -jnp.exp(A_log)
        y = _selective_scan(x_conv, delta, A, Bm, Cm, D_skip)
        y = y * jax.nn.silu(z)
        out = y @ W_out + b_out
        return _layernorm(residual + out, alpha, beta)

    def _L0_ffn_ref(x, weight, bias):
        import jax, jax.numpy as jnp
        import numpy as np
        FP8_E4M3_MAX = 448.0

        def fake_quant_fp8(t):
            amax = jnp.max(jnp.abs(t))
            scale = FP8_E4M3_MAX / jnp.maximum(amax, 1e-12)
            q = (t * scale).astype(jnp.float8_e4m3fn).astype(jnp.float32)
            return q / scale
        xq = fake_quant_fp8(x)
        wq = fake_quant_fp8(weight)
        return jnp.einsum('bsd,od->bso', xq, wq) + bias
    x = L0_attn_x
    x = x + _layernorm(_L0_attn_ref(_layernorm(x, axis=-1), L0_attn_W_in, L0_attn_b_in, L0_attn_conv_w, L0_attn_conv_b, L0_attn_W_xp, L0_attn_b_xp, L0_attn_W_dt, L0_attn_b_dt, L0_attn_A_log, L0_attn_D_skip, L0_attn_W_out, L0_attn_b_out, L0_attn_alpha, L0_attn_beta), axis=-1)
    x = x + _layernorm(_L0_ffn_ref(_layernorm(x, axis=-1), L0_ffn_weight, L0_ffn_bias), axis=-1)
    return x

_drawn_inputs = setup_inputs


def setup_inputs(seed=0):
    import zlib

    import numpy as np

    out = dict(_drawn_inputs(seed))
    spreads = {'L0_attn_b_in': (0.0, 0.8),
     'L0_attn_conv_b': (0.0, 0.8),
     'L0_attn_b_xp': (0.0, 0.8),
     'L0_attn_b_dt': (-1.0, 0.6),
     'L0_attn_D_skip': (1.0, 0.6),
     'L0_attn_b_out': (0.0, 0.1),
     'L0_attn_alpha': (1.0, 0.2),
     'L0_attn_beta': (0.0, 0.1)}
    factors = {'L0_attn_W_in': 8.0,
     'L0_attn_conv_w': 8.0,
     'L0_attn_W_xp': 8.0,
     'L0_attn_W_dt': 8.0,
     'L0_attn_A_log': 8.0,
     'L0_attn_W_out': 8.0,
     'L0_ffn_bias': 8.0}
    for name, (base, spread) in spreads.items():
        noise = np.random.default_rng([zlib.crc32(name.encode()), seed]).standard_normal(out[name].shape)
        drawn = base * np.exp(spread * noise) if base else spread * noise
        out[name] = jnp.asarray(drawn.astype(out[name].dtype))
    for name, factor in factors.items():
        out[name] = (out[name] * factor).astype(out[name].dtype)
    return out
```

```python
from contextlib import ExitStack

import concourse.bass as bass
from concourse import mybir

F32 = mybir.dt.float32
BF16 = mybir.dt.bfloat16
I32 = mybir.dt.int32
ALU = mybir.AluOpType
ACT = mybir.ActivationFunctionType
AX_X = mybir.AxisListType.X
ABSMAX = bass.bass_isa.ReduceOp.absmax

P = 128
DM = 128
DI = 256
HALVES = DI // P
DS = 16
TAPS = 4
L = 256
BATCH = 16
PAIR = 2
PAIRS = BATCH // PAIR
TC = L // P
CH = PAIR * TC
TOK = PAIR * L
SG = 2
UNITS = (DS // SG) * PAIR
BANK = 512

LAG_T, LAG_C, LAG_A = 1, 2, 3
DECAYS, DIAGS, STATES, TERMS = 2, 4, 4, 4
SUMS = UNITS - PAIR

LN_EPS = 1e-5
STD_EPS = 1e-6
FP8_MAX = 448.0
EXP_BITS = 0x7F800000
FP8_LEAST = 2.0 ** -6
ROUND_AT = 1.5 * 2.0 ** 20


class Pair:

    def __init__(self, value, least=None):
        self.v = value
        self.least = value if least is None else least

    def plus(self, k):
        return Pair(self.v + k, self.least + k)

    def after(self, d):
        if isinstance(self.v, int):
            return self.v >= d
        assert self.least >= d
        return True


def nth(pair, per, k):
    return pair.v * per + k


def trailing(pair, par, n, lag):
    if n >= lag:
        return pair, par, n - lag
    if not pair.after(1):
        return None
    return pair.plus(-1), 1 - par, n - lag + UNITS


def build_sandwich(nc, x, W_in, b_in, conv_w, conv_b, W_xp, b_xp, W_dt, b_dt, A_log, D_skip,
                   W_out, b_out, alpha, beta, ffn_w, ffn_b, out):
    ctx = ExitStack()
    with ctx:
        def sb(name, shape, dt=F32):
            return ctx.enter_context(nc.sbuf_tensor(name, shape, dt))

        def ps(name, shape):
            return ctx.enter_context(nc.psum_tensor(name, shape, F32))

        def sem(name):
            return ctx.enter_context(nc.semaphore(name))

        x_all = sb("x_all", [P, PAIRS * CH * DM])
        h2T = sb("h2T", [DM, PAIRS * TOK])
        w_in = sb("w_in", [P, 2 * DI])
        w_dt = sb("w_dt", [P, HALVES, DI])
        w_xp = sb("w_xp", [P, HALVES, 2 * DS])
        w_out = sb("w_out", [P, HALVES, DM])
        w_ffn = sb("w_ffn", [P, DM])
        w_ffnT = sb("w_ffnT", [P, DM])
        bin_c = sb("bin_c", [P, 2 * HALVES])
        cw = sb("cw", [P, HALVES, TAPS])
        cb = sb("cb", [P, HALVES])
        bdt = sb("bdt", [P, HALVES])
        dskip = sb("dskip", [P, HALVES])
        a_log = sb("a_log", [P, HALVES, DS])
        a_exp = sb("a_exp", [P, HALVES, DS])
        a_neg = sb("a_neg", [P, HALVES, DS])
        bxp_r = sb("bxp_r", [P, 2 * DS])
        bout_r = sb("bout_r", [P, DM])
        alpha_r = sb("alpha_r", [P, DM])
        beta_r = sb("beta_r", [P, DM])
        fb_r = sb("fb_r", [P, DM])
        ident = sb("ident", [P, P])
        minus_half = sb("minus_half", [P, CH])
        half = sb("half", [P, CH])

        st = sb("st", [P, CH, 6])
        mv = sb("mv", [P, CH, 2])
        var1 = sb("var1", [P, CH])
        rstd1 = sb("rstd1", [P, CH])
        xn = sb("xn", [P, CH * DM])
        xnb = sb("xnb", [P, 2, CH * DM])
        xnT = sb("xnT", [DM, TOK])
        xin = sb("xin", [P, HALVES, PAIR, TAPS - 1 + L])
        cv = sb("cv", [P, HALVES, PAIR, L])
        zv = sb("zv", [P, HALVES, TOK])
        xc = sb("xc", [P, 2, HALVES, TOK])
        sz = sb("sz", [P, 2, HALVES, TOK])
        dt_v = sb("dt_v", [P, HALVES, TOK])
        dt_e = sb("dt_e", [P, HALVES, TOK])
        delta = sb("delta", [P, 2, HALVES, PAIR, L])
        u = sb("u", [P, HALVES, TOK])
        uT = sb("uT", [P, 2, CH, DI])
        Bt = sb("Bt", [P, 2, DS // SG, PAIR, TC, SG])
        Ct = sb("Ct", [P, 2, CH, DS])

        decay = sb("decay", [P, DECAYS, HALVES, PAIR, SG, L])
        diag = sb("diag", [P, DIAGS, TC, SG, P])
        state = sb("state", [P, STATES, HALVES, SG, L])
        term = sb("term", [P, TERMS, TC, SG, DI])
        acc = sb("acc", [P, 2, PAIR, TC, SG, DI])
        ysumT = sb("ysumT", [P, CH, DI])

        yv = sb("yv", [P, HALVES, TOK])
        yg = sb("yg", [P, HALVES, TOK])
        res = sb("res", [P, CH * DM])
        nrm = sb("nrm", [P, CH * DM])
        bst = sb("bst", [P, CH, 6])
        bmv = sb("bmv", [P, CH, 2])
        bvar = sb("bvar", [P, CH])
        bstd = sb("bstd", [P, CH])
        bstd2 = sb("bstd2", [P, CH])
        bscale = sb("bscale", [P, CH])
        h2 = sb("h2", [P, CH * DM])
        amax_p = sb("amax_p", [P, PAIRS])
        amax_1 = sb("amax_1", [P, 1])

        wq_amax = sb("wq_amax", [P, 1])
        wq_all = sb("wq_all", [P, 1])
        wq_scale = sb("wq_scale", [P, 4])
        wq_m = sb("wq_m", [P, 3, DM])
        wqT = sb("wqT", [P, DM], BF16)
        x_amax = sb("x_amax", [P, 1])
        x_scale = sb("x_scale", [P, 4])
        xq = sb("xq", [P, 2, TOK], BF16)
        fst = sb("fst", [P, CH, 6])
        fmv = sb("fmv", [P, CH, 2])
        fvar = sb("fvar", [P, CH])
        frstd = sb("frstd", [P, 2, CH])
        fshift = sb("fshift", [P, 2, CH])
        state_flat = state[:, :, :, :, :].rearrange("p r h s t -> p (r h s t)")
        term_flat = term[:, :, :, :, :].rearrange("p r c s t -> p (r c s t)")
        tq, mq, rq, fo = (state_flat[:, 2 * TOK * k:2 * TOK * (k + 1)].rearrange("p (r n) -> p r n", r=2)
                          for k in range(4))
        ff, fn = (term_flat[:, 2 * TOK * k:2 * TOK * (k + 1)].rearrange("p (r n) -> p r n", r=2)
                  for k in range(2))

        drive = ps("drive", [P, 2, HALVES, SG * L])
        hT = ps("hT", [P, TC, SG * DI])
        fbank = ps("fbank", [P, BANK])
        bbank = ps("bbank", [P, BANK])

        dve_waited = sem("dve_waited")
        pool_waited = sem("pool_waited")
        x_first = sem("x_first")
        x_rest = sem("x_rest")
        w_loaded = sem("w_loaded")
        zeroed = sem("zeroed")
        ident_zero = sem("ident_zero")
        ident_ready = sem("ident_ready")
        consts_ready = sem("consts_ready")
        a_exp_ready = sem("a_exp_ready")
        a_neg_ready = sem("a_neg_ready")
        ln1_stats = sem("ln1_stats")
        ln1_mv = sem("ln1_mv")
        ln1_var = sem("ln1_var")
        ln1_rstd = sem("ln1_rstd")
        xn_ready = sem("xn_ready")
        xnb_ready = sem("xnb_ready")
        xnT_ready = sem("xnT_ready")
        front_full = sem("front_full")
        xin_ready = sem("xin_ready")
        conv_tap = sem("conv_tap")
        z_ready = sem("z_ready")
        xc_ready = sem("xc_ready")
        sz_ready = sem("sz_ready")
        dt_ready = sem("dt_ready")
        dt_neg = sem("dt_neg")
        sp_exp = sem("sp_exp")
        sp_log = sem("sp_log")
        delta_ready = sem("delta_ready")
        u_ready = sem("u_ready")
        bc_ready = sem("bc_ready")
        uT_ready = sem("uT_ready")
        decay_ready = sem("decay_ready")
        diag_ready = sem("diag_ready")
        drive_ready = sem("drive_ready")
        scan_done = sem("scan_done")
        hT_ready = sem("hT_ready")
        term_ready = sem("term_ready")
        sum_done = sem("sum_done")
        ysum_ready = sem("ysum_ready")
        back_full = sem("back_full")
        y_ready = sem("y_ready")
        gated = sem("gated")
        res_ready = sem("res_ready")
        b_step = sem("b_step")
        b_var = sem("b_var")
        b_root = sem("b_root")
        h2_ready = sem("h2_ready")
        h2T_ready = sem("h2T_ready")
        amax_ready = sem("amax_ready")
        wq_step = sem("wq_step")
        wq_full = sem("wq_full")
        wq_T = sem("wq_T")
        wq_local = sem("wq_local")
        wq_global = sem("wq_global")
        x_local = sem("x_local")
        x_global = sem("x_global")
        xs_step = sem("xs_step")
        t_ready = sem("t_ready")
        m_step = sem("m_step")
        r_ready = sem("r_ready")
        xq_ready = sem("xq_ready")
        f_full = sem("f_full")
        f_ready = sem("f_ready")
        f_stats = sem("f_stats")
        f_mv = sem("f_mv")
        f_var = sem("f_var")
        f_rstd = sem("f_rstd")
        f_shift = sem("f_shift")
        f_norm = sem("f_norm")
        f_out = sem("f_out")
        stored = [sem("stored_even"), sem("stored_odd")]

        x_v = x.rearrange("b l d -> (b l) d").rearrange("(k p) d -> p k d", p=P)
        out_v = out.rearrange("b l d -> (b l) d").rearrange("(k p) d -> p k d", p=P)
        x_k = x_all[:, :].rearrange("p (k d) -> p k d", d=DM)
        W_LOADS = 16
        B_STEPS = 13
        block = ctx.enter_context(nc.Block())

        def chunks(t):
            return t.rearrange("p (j d) -> p j d", d=DM)

        def on_chunks(row):
            return row.unsqueeze(1).to_broadcast([P, CH, row.shape[-1]])

        def column(vector):
            return vector.rearrange("(h p) -> p h", p=P)

        def row(vector):
            return vector.rearrange("(a n) -> a n", a=1).to_broadcast([P, vector.shape[0]])

        @block.sync
        def _(sp):
            sp.dma_start(x_k[:, 0:CH, :], x_v[:, 0:CH, :]).then_inc(x_first, 16)
            sp.dma_start(w_in[:, :], W_in).then_inc(w_loaded, 16)
            sp.dma_start(bin_c[:, :], column(b_in), allow_slow_non_contiguous=True).then_inc(w_loaded, 16)
            sp.dma_start(cw[:, :, :], conv_w.rearrange("(h p) a k -> p h (a k)", p=P)).then_inc(w_loaded, 16)
            sp.dma_start(cb[:, :], column(conv_b), allow_slow_non_contiguous=True).then_inc(w_loaded, 16)
            sp.dma_start(w_dt[:, :, :], W_dt.rearrange("(h p) n -> p h n", p=P)).then_inc(w_loaded, 16)
            sp.dma_start(bdt[:, :], column(b_dt), allow_slow_non_contiguous=True).then_inc(w_loaded, 16)
            sp.dma_start(a_log[:, :, :], A_log.rearrange("(h p) n -> p h n", p=P)).then_inc(w_loaded, 16)
            sp.dma_start(w_xp[:, :, :], W_xp.rearrange("(h p) n -> p h n", p=P)).then_inc(w_loaded, 16)
            sp.dma_start(bxp_r[:, :], row(b_xp)).then_inc(w_loaded, 16)
            sp.dma_start(dskip[:, :], column(D_skip), allow_slow_non_contiguous=True).then_inc(w_loaded, 16)
            sp.dma_start(w_out[:, :, :], W_out.rearrange("(h p) n -> p h n", p=P)).then_inc(w_loaded, 16)
            sp.dma_start(bout_r[:, :], row(b_out)).then_inc(w_loaded, 16)
            sp.dma_start(alpha_r[:, :], row(alpha)).then_inc(w_loaded, 16)
            sp.dma_start(beta_r[:, :], row(beta)).then_inc(w_loaded, 16)
            sp.dma_start(fb_r[:, :], row(ffn_b)).then_inc(w_loaded, 16)
            sp.dma_start(w_ffn[:, :], ffn_w).then_inc(w_loaded, 16)
            sp.dma_start(x_k[:, CH:, :], x_v[:, CH:, :]).then_inc(x_rest, 16)
            with sp.Fori(0, PAIRS // 2) as i:
                for par in range(2):
                    grp = Pair(i * 2 + par, par)
                    sp.wait_ge(f_out, nth(grp, 1, 1))
                    sp.dma_start(out_v[:, bass.ds(grp.v * CH, CH), :], chunks(fo[:, par, :])).then_inc(stored[par], 16)
            for par in range(2):
                sp.wait_ge(stored[par], 16 * PAIRS // 2)

        @block.gpsimd
        def _(pool):
            pool.memset(ident[:, :], 0.0).then_inc(ident_zero, 1)
            pool.memset(minus_half[:, :], -0.5).then_inc(consts_ready, 1)
            pool.memset(half[:, :], 0.5).then_inc(consts_ready, 1)
            pool.wait_ge(ident_zero, 1)
            pool.affine_select(out=ident[:, :], in_=ident[:, :], compare_op=ALU.not_equal, fill=1.0, base=0,
                               pattern=[[-1, P]], channel_multiplier=1).then_inc(ident_ready, 1)
            pool.wait_ge(consts_ready, 2)

            def front_root(pr):
                pool.wait_ge(ln1_var, nth(pr, 1, 1))
                nc.gpsimd.tensor_tensor(rstd1[:, :], var1[:, :], minus_half[:, :], ALU.pow).then_inc(ln1_rstd, 1)

            def front_residual(pr, par):
                pool.wait_ge(xn_ready, nth(pr, 1, 1))
                if pr.after(2):
                    pool.wait_ge(res_ready, nth(pr.plus(-1), 1, 0))
                if not pr.after(1):
                    pool.wait_ge(w_loaded, 16 * W_LOADS)
                nc.gpsimd.tensor_tensor(chunks(xnb[:, par, :]), chunks(xn[:, :]), on_chunks(bout_r[:, :]), ALU.add)\
                    .then_inc(xnb_ready, 1)

            def diag_b(pr, par, n):
                g, b = n // PAIR, n % PAIR
                if n == 0:
                    pool.wait_ge(bc_ready, nth(pr, 3, 2))
                old = trailing(pr, par, n, DIAGS)
                if old:
                    pool.wait_ge(drive_ready, nth(old[0], 2 * UNITS, 2 * old[2] + 2))
                pool.sem_inc(pool_waited, 1)
                b_cols = Bt[:, par, g, b, :, :].rearrange("p c s -> p (c s)").unsqueeze(2).to_broadcast([P, TC * SG, P])
                nc.gpsimd.affine_select(out=diag[:, n % DIAGS, :, :, :].rearrange("p c s t -> p (c s) t"), in_=b_cols,
                                        compare_op=ALU.is_equal, fill=0.0, base=0, pattern=[[0, TC * SG], [-1, P]],
                                        channel_multiplier=1).then_inc(diag_ready, 1)

            def add_terms(pr, par, n):
                g, b = n // PAIR, n % PAIR
                if g == 0:
                    return
                pool.wait_ge(term_ready, nth(pr, 2 * UNITS, 2 * n + 2))
                if g > 1:
                    pool.wait_ge(sum_done, nth(pr, SUMS, n - 2 * PAIR + 1))
                a = acc[:, par, b, :, :, :]
                nc.gpsimd.tensor_tensor(a, a, term[:, n % TERMS, :, :, :], ALU.add).then_inc(sum_done, 1)

            def sum_states(pr, par):
                pool.wait_ge(sum_done, nth(pr, SUMS, SUMS))
                for b in range(PAIR):
                    nc.gpsimd.tensor_tensor(ysumT[:, TC * b:TC * b + TC, :], acc[:, par, b, :, 0, :],
                                            acc[:, par, b, :, 1, :], ALU.add).then_inc(ysum_ready, 1)

            def back_root(pr, k):
                pool.wait_ge(b_var, nth(pr, 3, k + 1))
                nc.gpsimd.tensor_tensor(bstd[:, :], bvar[:, :], (half if k == 0 else minus_half)[:, :], ALU.pow)\
                    .then_inc(b_root, 1)

            def slot(pr, par, front, back, units=UNITS):
                for n in range(units):
                    if units == UNITS:
                        diag_b(pr, par, n)
                    old = trailing(pr, par, n, LAG_A)
                    if old:
                        add_terms(*old)
                    nxt, npar, prv, ppar = pr.plus(1), 1 - par, pr.plus(-1), 1 - par
                    if front:
                        if n == 0:
                            front_root(nxt)
                        if n == 10:
                            front_residual(nxt, npar)
                    if back:
                        if n == 4:
                            sum_states(prv, ppar)
                        if n in (8, 10, 12):
                            back_root(prv, (n - 8) // 2)

            front_root(Pair(0))
            front_residual(Pair(0), 0)
            pool.wait_ge(wq_local, 1)
            nc.gpsimd.partition_all_reduce(wq_all[:, :], wq_amax[:, :], P, ABSMAX).then_inc(wq_global, 1)
            slot(Pair(0), 0, True, False)
            with pool.Fori(0, (PAIRS - 2) // 2) as i:
                for k in range(2):
                    slot(Pair(i * 2 + (1 + k), 1 + k), 1 - k, True, True)
            slot(Pair(PAIRS - 1), 1, False, True)
            slot(Pair(PAIRS), 0, False, False, LAG_A)
            sum_states(Pair(PAIRS - 1), 1)
            for k in range(3):
                back_root(Pair(PAIRS - 1), k)

            pool.wait_ge(x_local, 1)
            nc.gpsimd.partition_all_reduce(x_amax[:, :], amax_1[:, :], P, ABSMAX).then_inc(x_global, 1)

            def round_up(grp, par):
                pool.wait_ge(t_ready, nth(grp, 1, 1))
                pool.wait_ge(m_step, nth(grp, 2, 2))
                nc.gpsimd.tensor_tensor(rq[:, par, :], tq[:, par, :], mq[:, par, :], ALU.add).then_inc(r_ready, 1)

            def last_root(grp, par):
                pool.wait_ge(f_var, nth(grp, 1, 1))
                nc.gpsimd.tensor_tensor(frstd[:, par, :], fvar[:, :], minus_half[:, :], ALU.pow).then_inc(f_rstd, 1)

            def last_sum(grp, par):
                pool.wait_ge(f_norm, nth(grp, 1, 1))
                if grp.after(2):
                    pool.wait_ge(stored[par], (grp.v - par) * 8)
                nc.gpsimd.tensor_tensor(fo[:, par, :], fn[:, par, :], x_all[:, bass.ds(grp.v * TOK, TOK)], ALU.add)\
                    .then_inc(f_out, 1)

            def tail(grp, par, new=True, old=True):
                if new:
                    round_up(grp, par)
                if old:
                    last_root(grp.plus(-1), 1 - par)
                    last_sum(grp.plus(-1), 1 - par)

            tail(Pair(0), 0, old=False)
            tail(Pair(1), 1)
            tail(Pair(2), 0)
            with pool.Fori(1, PAIRS // 2 - 1) as i:
                for k in range(2):
                    tail(Pair(i * 2 + (1 + k), 3 + k), 1 - k)
            tail(Pair(PAIRS - 1), 1)
            tail(Pair(PAIRS), 0, new=False)

        @block.scalar
        def _(act):
            def front_xnT(pr):
                act.wait_ge(front_full, nth(pr, 10, 1))
                nc.scalar.activation(xnT[:, :], fbank[:, :], ACT.Copy).then_inc(xnT_ready, 1)

            def front_xin(pr, h):
                act.wait_ge(front_full, nth(pr, 10, 2 + h))
                if pr.after(1):
                    act.wait_ge(conv_tap, nth(pr.plus(-1), 2 * TAPS, TAPS * (h + 1)))
                nc.scalar.activation(xin[:, h, :, TAPS - 1:], fbank[:, :].rearrange("p (b t) -> p b t", b=PAIR),
                                     ACT.Identity, bias=bin_c[:, h:h + 1]).then_inc(xin_ready, 1)

            def front_silu_x(pr, par):
                act.wait_ge(conv_tap, nth(pr, 2 * TAPS, 2 * TAPS))
                if pr.after(2):
                    act.wait_ge(y_ready, nth(pr.plus(-2), 2, 2))
                nc.scalar.activation(xc[:, par, :, :], cv[:, :, :, :].rearrange("p h b t -> p h (b t)"), ACT.Silu)\
                    .then_inc(xc_ready, 1)

            def front_silu_z(pr, par):
                act.wait_ge(z_ready, nth(pr, 2, 2))
                if pr.after(2):
                    act.wait_ge(gated, nth(pr.plus(-2), 1, 1))
                nc.scalar.activation(sz[:, par, :, :], zv[:, :, :], ACT.Silu).then_inc(sz_ready, 1)

            def front_softplus(pr):
                act.wait_ge(dt_neg, nth(pr, 1, 1))
                nc.scalar.activation(dt_e[:, :, :], dt_e[:, :, :], ACT.Exp).then_inc(sp_exp, 1)
                act.wait_ge(sp_exp, nth(pr, 1, 1))
                nc.scalar.activation(dt_e[:, :, :], dt_e[:, :, :], ACT.Ln, bias=1.0).then_inc(sp_log, 1)

            def front_uT(pr, par, k):
                act.wait_ge(front_full, nth(pr, 10, 9 + k))
                nc.scalar.activation(uT[:, par, 2 * k:2 * k + 2, :],
                                     fbank[:, :].rearrange("p (j d) -> p j d", d=DI), ACT.Copy).then_inc(uT_ready, 1)

            def exp_decay(pr, par, g):
                if g == 0:
                    act.wait_ge(delta_ready, nth(pr, 1, 1))
                old = trailing(pr, par, PAIR * g + 1, PAIR * DECAYS)
                if old:
                    act.wait_ge(scan_done, nth(old[0], 2 * UNITS, 2 * old[2] + 2))
                for h in range(HALVES):
                    for s in range(SG):
                        last = nc.scalar.activation(decay[:, g % DECAYS, h, :, s, 1:], delta[:, par, h, :, 1:],
                                                    ACT.Exp, scale=a_neg[:, h, SG * g + s:SG * g + s + 1])
                last.then_inc(decay_ready, 1)

            def scale_c(pr, par, n):
                g, b = n // PAIR, n % PAIR
                if g > 0:
                    old = trailing(pr, par, n, TERMS)
                    if old and old[2] >= PAIR:
                        act.wait_ge(sum_done, nth(old[0], SUMS, old[2] - PAIR + 1))
                if n == 0:
                    act.wait_ge(bc_ready, nth(pr, 3, 3))
                for c in range(TC):
                    act.wait_ge(hT_ready, nth(pr, 2 * UNITS, 2 * n + c + 1))
                    for s in range(SG):
                        dst = acc[:, par, b, c, s, :] if g == 0 else term[:, n % TERMS, c, s, :]
                        last = nc.scalar.activation(dst, hT[:, c, DI * s:DI * s + DI], ACT.Copy,
                                                    scale=Ct[:, par, TC * b + c, SG * g + s:SG * g + s + 1])
                    last.then_inc(term_ready, 1)

            def back_h2T(pr):
                act.wait_ge(back_full, nth(pr, 4, 4))
                nc.scalar.activation(h2T[:, bass.ds(pr.v * TOK, TOK)], bbank[:, :], ACT.Copy).then_inc(h2T_ready, 1)

            def slot(pr, par, front, back, units=UNITS):
                for n in range(units):
                    if units == UNITS and n % PAIR == 0:
                        exp_decay(pr, par, n // PAIR)
                    old = trailing(pr, par, n, LAG_C)
                    if old:
                        scale_c(*old)
                    nxt, npar, prv = pr.plus(1), 1 - par, pr.plus(-1)
                    if front:
                        if n == 2:
                            front_xnT(nxt)
                        if n in (3, 4):
                            front_xin(nxt, n - 3)
                        if n == 7:
                            front_silu_x(nxt, npar)
                        if n == 8:
                            front_silu_z(nxt, npar)
                        if n == 10:
                            front_softplus(nxt)
                        if n in (12, 13):
                            front_uT(nxt, npar, n - 12)
                    if back and n == 14:
                        back_h2T(prv)

            act.wait_ge(w_loaded, 16 * W_LOADS)
            nc.scalar.activation(a_exp[:, :, :], a_log[:, :, :], ACT.Exp).then_inc(a_exp_ready, 1)
            act.wait_ge(zeroed, 2)
            front_xnT(Pair(0))
            for h in range(HALVES):
                front_xin(Pair(0), h)
            front_silu_x(Pair(0), 0)
            front_silu_z(Pair(0), 0)
            front_softplus(Pair(0))
            for k in range(2):
                front_uT(Pair(0), 0, k)
            act.wait_ge(a_neg_ready, 1)
            
            slot(Pair(0), 0, True, False)
            with act.Fori(0, (PAIRS - 2) // 2) as i:
                for k in range(2):
                    slot(Pair(i * 2 + (1 + k), 1 + k), 1 - k, True, True)
            slot(Pair(PAIRS - 1), 1, False, True)
            slot(Pair(PAIRS), 0, False, False, LAG_C)
            back_h2T(Pair(PAIRS - 1))

            def scale_x(grp, par):
                if grp.after(2):
                    act.wait_ge(r_ready, grp.v - 1)
                nc.scalar.activation(tq[:, par, :], h2T[:, bass.ds(grp.v * TOK, TOK)], ACT.Copy,
                                     scale=x_scale[:, 1:2]).then_inc(t_ready, 1)

            def last_norm(grp, par):
                act.wait_ge(f_shift, nth(grp, 1, 1))
                if grp.after(2):
                    act.wait_ge(f_out, grp.v - 1)
                for j in range(CH):
                    last = nc.scalar.activation(fn[:, par, DM * j:DM * j + DM], ff[:, par, DM * j:DM * j + DM],
                                                ACT.Identity, bias=fshift[:, par, j:j + 1],
                                                scale=frstd[:, par, j:j + 1])
                last.then_inc(f_norm, 1)

            def tail(grp, par, new=True, old=True):
                if new:
                    scale_x(grp, par)
                if old:
                    last_norm(grp.plus(-2), par)

            act.wait_ge(xs_step, 3)
            tail(Pair(0), 0, old=False)
            tail(Pair(1), 1, old=False)
            tail(Pair(2), 0)
            tail(Pair(3), 1)
            with act.Fori(2, PAIRS // 2) as i:
                for k in range(2):
                    tail(Pair(i * 2 + k, 4 + k), k)
            tail(Pair(PAIRS), 0, new=False)
            tail(Pair(PAIRS + 1), 1, new=False)

        @block.tensor
        def _(pe):
            front_read = [(xnT_ready, 1, 1), (xin_ready, 2, 1), (xin_ready, 2, 2), (z_ready, 2, 1), (z_ready, 2, 2),
                          (dt_ready, 2, 1), (dt_ready, 2, 2), (bc_ready, 3, 3), (uT_ready, 2, 1), (uT_ready, 2, 2)]
            back_read = [(y_ready, 2, 1), (y_ready, 2, 2), (res_ready, 1, 1), (h2T_ready, 1, 1)]

            def bank_free(reads, pr, k):
                if k == 0 and (reads is back_read or not pr.after(1)):
                    return
                signal, per, count = reads[k - 1]
                pe.wait_ge(signal, nth(pr, per, count if k else 0))

            def front_transpose(pr):
                pe.wait_ge(xn_ready, nth(pr, 1, 1))
                bank_free(front_read, pr, 0)
                for j in range(CH):
                    last = nc.tensor.transpose(fbank[:, P * j:P * j + P], xn[:, DM * j:DM * j + DM], ident[:, :])
                last.then_inc(front_full, 1)

            def front_in(pr, k):
                if k == 0:
                    pe.wait_ge(xnT_ready, nth(pr, 1, 1))
                bank_free(front_read, pr, 1 + k)
                nc.tensor.matmul(fbank[:, :], w_in[:, P * k:P * k + P], xnT[:, :], start=True, stop=True)\
                    .then_inc(front_full, 1)

            def front_dt(pr, par, m):
                if m == 0:
                    pe.wait_ge(xc_ready, nth(pr, 1, 1))
                bank_free(front_read, pr, 5 + m)
                for h in range(HALVES):
                    last = nc.tensor.matmul(fbank[:, :], w_dt[:, h, P * m:P * m + P], xc[:, par, h, :],
                                            start=(h == 0), stop=(h == HALVES - 1))
                last.then_inc(front_full, 1)

            def front_bc(pr, par):
                bank_free(front_read, pr, 7)
                for j in range(CH):
                    for h in range(HALVES):
                        last = nc.tensor.matmul(fbank[:, 2 * DS * j:2 * DS * (j + 1)], xc[:, par, h, P * j:P * j + P],
                                                w_xp[:, h, :], start=(h == 0), stop=(h == HALVES - 1))
                last.then_inc(front_full, 1)

            def front_ut(pr, k):
                if k == 0:
                    pe.wait_ge(u_ready, nth(pr, 1, 1))
                bank_free(front_read, pr, 8 + k)
                for jj in range(2):
                    j = 2 * k + jj
                    for h in range(HALVES):
                        last = nc.tensor.transpose(fbank[:, DI * jj + P * h:DI * jj + P * h + P],
                                                   u[:, h, P * j:P * j + P], ident[:, :])
                last.then_inc(front_full, 1)

            def drive_unit(pr, par, n):
                b = n % PAIR
                if n == 0:
                    pe.wait_ge(uT_ready, nth(pr, 2, 2))
                pe.wait_ge(diag_ready, nth(pr, UNITS, n + 1))
                old = trailing(pr, par, n, 2)
                for h in range(HALVES):
                    if old:
                        pe.wait_ge(scan_done, nth(old[0], 2 * UNITS, 2 * old[2] + h + 1))
                    dst = drive[:, n % 2, h, :].rearrange("p (s t) -> p s t", s=SG)
                    for c in range(TC):
                        last = nc.tensor.matmul(dst[:, :, P * c:P * c + P], uT[:, par, TC * b + c, P * h:P * h + P],
                                                diag[:, n % DIAGS, c, :, :], start=True, stop=True)
                    last.then_inc(drive_ready, 1)

            def transpose_states(pr, par, n):
                pe.wait_ge(scan_done, nth(pr, 2 * UNITS, 2 * n + 2))
                old = trailing(pr, par, n, 1)
                for c in range(TC):
                    if old:
                        pe.wait_ge(term_ready, nth(old[0], 2 * UNITS, 2 * old[2] + c + 1))
                    for s in range(SG):
                        for h in range(HALVES):
                            last = nc.tensor.transpose(hT[:, c, DI * s + P * h:DI * s + P * h + P],
                                                       state[:, n % STATES, h, s, P * c:P * c + P], ident[:, :])
                    last.then_inc(hT_ready, 1)

            def back_y(pr, h):
                if h == 0:
                    pe.wait_ge(ysum_ready, nth(pr, 2, 2))
                bank_free(back_read, pr, h)
                for j in range(CH):
                    last = nc.tensor.transpose(bbank[:, P * j:P * j + P], ysumT[:, j, P * h:P * h + P], ident[:, :])
                last.then_inc(back_full, 1)

            def back_out(pr):
                pe.wait_ge(gated, nth(pr, 1, 1))
                bank_free(back_read, pr, 2)
                for j in range(CH):
                    for h in range(HALVES):
                        last = nc.tensor.matmul(bbank[:, DM * j:DM * j + DM], yg[:, h, P * j:P * j + P],
                                                w_out[:, h, :], start=(h == 0), stop=(h == HALVES - 1))
                last.then_inc(back_full, 1)

            def back_transpose(pr):
                pe.wait_ge(h2_ready, nth(pr, 1, 1))
                bank_free(back_read, pr, 3)
                for j in range(CH):
                    last = nc.tensor.transpose(bbank[:, P * j:P * j + P], h2[:, DM * j:DM * j + DM], ident[:, :])
                last.then_inc(back_full, 1)

            def slot(pr, par, front, back, units=UNITS):
                for n in range(units):
                    if units == UNITS:
                        drive_unit(pr, par, n)
                    old = trailing(pr, par, n, LAG_T)
                    if old:
                        transpose_states(*old)
                    nxt, npar, prv = pr.plus(1), 1 - par, pr.plus(-1)
                    if front:
                        if n == 2:
                            front_transpose(nxt)
                        if 3 <= n < 7:
                            front_in(nxt, n - 3)
                        if n in (8, 9):
                            front_dt(nxt, npar, n - 8)
                        if n == 10:
                            front_bc(nxt, npar)
                        if n in (12, 13):
                            front_ut(nxt, n - 12)
                    if back:
                        if n in (5, 6):
                            back_y(prv, n - 5)
                        if n == 8:
                            back_out(prv)
                        if n == 14:
                            back_transpose(prv)

            pe.wait_ge(ident_ready, 1)
            pe.wait_ge(w_loaded, 16 * W_LOADS)
            front_transpose(Pair(0))
            for k in range(2 * HALVES):
                front_in(Pair(0), k)
            for m in range(HALVES):
                front_dt(Pair(0), 0, m)
            front_bc(Pair(0), 0)
            for k in range(2):
                front_ut(Pair(0), k)
            nc.tensor.transpose(bbank[:, 0:P], w_ffn[:, :], ident[:, :]).then_inc(wq_full, 1)
            slot(Pair(0), 0, True, False)
            pe.wait_ge(wq_T, 1)
            with pe.Fori(0, (PAIRS - 2) // 2) as i:
                for k in range(2):
                    slot(Pair(i * 2 + (1 + k), 1 + k), 1 - k, True, True)
            slot(Pair(PAIRS - 1), 1, False, True)
            slot(Pair(PAIRS), 0, False, False, LAG_T)
            last_pair = Pair(PAIRS - 1)
            for h in range(HALVES):
                back_y(last_pair, h)
            back_out(last_pair)
            back_transpose(last_pair)

            def tail(grp, par):
                pe.wait_ge(xq_ready, nth(grp, 1, 1))
                if grp.after(2):
                    pe.wait_ge(f_ready, grp.v - 1)
                for j in range(CH):
                    last = nc.tensor.matmul(drive[:, par, 0, DM * j:DM * j + DM], xq[:, par, P * j:P * j + P],
                                            wqT[:, :], start=True, stop=True)
                last.then_inc(f_full, 1)

            tail(Pair(0), 0)
            tail(Pair(1), 1)
            with pe.Fori(1, PAIRS // 2) as i:
                for k in range(2):
                    tail(Pair(i * 2 + k, 2 + k), k)

        @block.vector
        def _(dve):
            def front_stats(pr):
                if not pr.after(1):
                    dve.wait_ge(x_first, 16)
                elif isinstance(pr.v, int) and pr.v == 1:
                    dve.wait_ge(x_rest, 16)
                for j in range(CH):
                    nc.vector.bn_stats(st[:, j, :], x_all[:, bass.ds(pr.v * TOK + DM * j, DM)]).then_inc(ln1_stats, 1)
                dve.wait_ge(ln1_stats, nth(pr, CH, CH))
                dve.sem_inc(dve_waited, 1)
                for j in range(CH):
                    nc.vector.bn_aggr(mv[:, j, :], st[:, j, :]).then_inc(ln1_mv, 1)
                dve.wait_ge(ln1_mv, nth(pr, CH, CH))
                nc.vector.tensor_scalar(var1[:, :], mv[:, :, 1], LN_EPS, None, ALU.add).then_inc(ln1_var, 1)

            def front_norm(pr):
                dve.wait_ge(ln1_rstd, nth(pr, 1, 1))
                if pr.after(1):
                    dve.wait_ge(xnb_ready, nth(pr, 1, 0))
                for j in range(CH):
                    last = nc.vector.tensor_scalar(xn[:, DM * j:DM * j + DM],
                                                   x_all[:, bass.ds(pr.v * TOK + DM * j, DM)],
                                                   mv[:, j, 0:1], rstd1[:, j:j + 1], ALU.subtract, ALU.mult)
                last.then_inc(xn_ready, 1)

            def front_conv(pr, h):
                dve.wait_ge(xin_ready, nth(pr, 2, h + 1))
                y = cv[:, h, :, :]
                nc.vector.tensor_scalar(y, xin[:, h, :, 0:L], cw[:, h, 0:1], cb[:, h:h + 1], ALU.mult, ALU.add)\
                    .then_inc(conv_tap, 1)
                for k in range(1, TAPS):
                    dve.wait_ge(conv_tap, nth(pr, 2 * TAPS, TAPS * h + k))
                    nc.vector.scalar_tensor_tensor(out=y, in0=xin[:, h, :, k:k + L], scalar=cw[:, h, k:k + 1],
                                                   in1=y, op0=ALU.mult, op1=ALU.add).then_inc(conv_tap, 1)

            def front_z(pr, h):
                dve.wait_ge(front_full, nth(pr, 10, 4 + h))
                nc.vector.tensor_scalar(zv[:, h, :], fbank[:, :], bin_c[:, HALVES + h:HALVES + h + 1], None, ALU.add)\
                    .then_inc(z_ready, 1)

            def front_dt(pr, m):
                dve.wait_ge(front_full, nth(pr, 10, 6 + m))
                nc.vector.tensor_scalar(dt_v[:, m, :], fbank[:, :], bdt[:, m:m + 1], None, ALU.add)\
                    .then_inc(dt_ready, 1)
                if m == HALVES - 1:
                    dve.wait_ge(dt_ready, nth(pr, 2, 2))
                    nc.vector.scalar_tensor_tensor(out=dt_e[:, :, :], in0=dt_v[:, :, :], scalar=-1.0,
                                                   in1=dt_v[:, :, :], op0=ALU.mult, op1=ALU.min).then_inc(dt_neg, 1)

            def front_bc(pr, par):
                dve.wait_ge(front_full, nth(pr, 10, 8))
                bc = fbank[:, 0:CH * 2 * DS].rearrange("p (b c n) -> p b c n", b=PAIR, c=TC)
                bias = bxp_r[:, 0:DS].rearrange("p (g s) -> p g s", s=SG).unsqueeze(1).to_broadcast([P, TC, DS // SG, SG])
                for b in range(PAIR):
                    nc.vector.tensor_tensor(Bt[:, par, :, b, :, :].rearrange("p g c s -> p c g s"),
                                            bc[:, b, :, 0:DS].rearrange("p c (g s) -> p c g s", s=SG), bias, ALU.add)\
                        .then_inc(bc_ready, 1)
                nc.vector.tensor_tensor(Ct[:, par, :, :], bc[:, :, :, DS:].rearrange("p b c n -> p (b c) n"),
                                        on_chunks(bxp_r[:, DS:]), ALU.add).then_inc(bc_ready, 1)

            def front_delta(pr, par):
                dve.wait_ge(sp_log, nth(pr, 1, 1))
                d = delta[:, par, :, :, :].rearrange("p h b t -> p h (b t)")
                nc.vector.scalar_tensor_tensor(out=d, in0=dt_v[:, :, :], scalar=0.0, in1=dt_e[:, :, :],
                                               op0=ALU.max, op1=ALU.add).then_inc(delta_ready, 1)
                dve.wait_ge(delta_ready, nth(pr, 1, 1))
                nc.vector.tensor_tensor(u[:, :, :], d, xc[:, par, :, :], ALU.mult).then_inc(u_ready, 1)

            def scan_unit(pr, par, n):
                g, b = n // PAIR, n % PAIR
                if b == 0:
                    dve.wait_ge(decay_ready, nth(pr, UNITS // PAIR, g + 1))
                old = trailing(pr, par, n, STATES)
                if old:
                    dve.wait_ge(hT_ready, nth(old[0], 2 * UNITS, 2 * old[2] + 2))
                for h in range(HALVES):
                    dve.wait_ge(drive_ready, nth(pr, 2 * UNITS, 2 * n + h + 1))
                    nc.vector.tensor_tensor_scan(state[:, n % STATES, h, :, :].rearrange("p s t -> p (s t)"),
                                                 decay[:, g % DECAYS, h, b, :, :].rearrange("p s t -> p (s t)"),
                                                 drive[:, n % 2, h, :], 0.0, ALU.mult, ALU.add).then_inc(scan_done, 1)

            def back_y(pr, par, h):
                dve.wait_ge(back_full, nth(pr, 4, h + 1))
                nc.vector.scalar_tensor_tensor(out=yv[:, h, :], in0=xc[:, par, h, :], scalar=dskip[:, h:h + 1],
                                               in1=bbank[:, :], op0=ALU.mult, op1=ALU.add).then_inc(y_ready, 1)

            def back_gate(pr, par):
                dve.wait_ge(y_ready, nth(pr, 2, 2))
                nc.vector.tensor_tensor(yg[:, :, :], yv[:, :, :], sz[:, par, :, :], ALU.mult).then_inc(gated, 1)

            def b_wait(pr, k):
                dve.wait_ge(b_step, nth(pr, B_STEPS, k))

            def stats_of(pr, src, k):
                for j in range(CH):
                    last = nc.vector.bn_stats(bst[:, j, :], src(j))
                last.then_inc(b_step, 1)
                b_wait(pr, k + 1)
                dve.sem_inc(dve_waited, 1)
                for j in range(CH):
                    last = nc.vector.bn_aggr(bmv[:, j, :], bst[:, j, :])
                last.then_inc(b_step, 1)
                b_wait(pr, k + 2)

            def normalize(dst, src, rs):
                for j in range(CH):
                    last = nc.vector.tensor_scalar(dst(j), src(j), bmv[:, j, 0:1], rs[:, j:j + 1],
                                                   ALU.subtract, ALU.mult)
                return last

            def part(t):
                return lambda j: t[:, DM * j:DM * j + DM]

            def back_norm_a(pr, par):
                dve.wait_ge(back_full, nth(pr, 4, 3))
                dve.wait_ge(xnb_ready, nth(pr, 1, 1))
                nc.vector.tensor_tensor(res[:, :], bbank[:, :], xnb[:, par, :], ALU.add).then_inc(res_ready, 1)
                dve.wait_ge(res_ready, nth(pr, 1, 1))
                stats_of(pr, part(res), 0)
                nc.vector.tensor_scalar(bvar[:, :], bmv[:, :, 1], DM / (DM - 1.0), None, ALU.mult).then_inc(b_var, 1)

            def back_norm_b(pr):
                dve.wait_ge(b_root, nth(pr, 3, 1))
                nc.vector.tensor_scalar(bstd2[:, :], bstd[:, :], STD_EPS, None, ALU.add).then_inc(b_step, 1)
                b_wait(pr, 3)
                nc.vector.reciprocal(bscale[:, :], bstd2[:, :]).then_inc(b_step, 1)
                b_wait(pr, 4)
                normalize(part(nrm), part(res), bscale).then_inc(b_step, 1)
                b_wait(pr, 5)
                nc.vector.tensor_tensor(chunks(nrm[:, :]), chunks(nrm[:, :]), on_chunks(alpha_r[:, :]), ALU.mult)\
                    .then_inc(b_step, 1)
                b_wait(pr, 6)
                nc.vector.tensor_tensor(chunks(nrm[:, :]), chunks(nrm[:, :]), on_chunks(beta_r[:, :]), ALU.add)\
                    .then_inc(b_step, 1)
                b_wait(pr, 7)
                stats_of(pr, part(nrm), 7)
                nc.vector.tensor_scalar(bvar[:, :], bmv[:, :, 1], LN_EPS, None, ALU.add).then_inc(b_var, 1)

            def back_norm_c(pr):
                dve.wait_ge(b_root, nth(pr, 3, 2))
                normalize(part(nrm), part(nrm), bstd).then_inc(b_step, 1)
                b_wait(pr, 10)
                x1 = x_all[:, bass.ds(pr.v * TOK, TOK)]
                nc.vector.tensor_tensor(x1, x1, nrm[:, :], ALU.add).then_inc(b_step, 1)
                b_wait(pr, 11)
                dve.sem_inc(dve_waited, 1)
                stats_of(pr, lambda j: x_all[:, bass.ds(pr.v * TOK + DM * j, DM)], 11)
                nc.vector.tensor_scalar(bvar[:, :], bmv[:, :, 1], LN_EPS, None, ALU.add).then_inc(b_var, 1)

            def back_norm_d(pr):
                dve.wait_ge(b_root, nth(pr, 3, 3))
                normalize(part(h2), lambda j: x_all[:, bass.ds(pr.v * TOK + DM * j, DM)], bstd).then_inc(h2_ready, 1)

            def back_amax(pr):
                dve.wait_ge(h2T_ready, nth(pr, 1, 1))
                nc.vector.tensor_reduce(amax_p[:, bass.ds(pr.v, 1)], h2T[:, bass.ds(pr.v * TOK, TOK)], AX_X, ALU.max,
                                        apply_absolute_value=True).then_inc(amax_ready, 1)

            def slot(pr, par, front, back):
                for n in range(UNITS):
                    scan_unit(pr, par, n)
                    nxt, npar, prv, ppar = pr.plus(1), 1 - par, pr.plus(-1), 1 - par
                    if front:
                        if n == 0:
                            front_stats(nxt)
                        if n == 1:
                            front_norm(nxt)
                        if n in (4, 5):
                            front_conv(nxt, n - 4)
                        if n in (5, 6):
                            front_z(nxt, n - 5)
                        if n in (8, 9):
                            front_dt(nxt, n - 8)
                        if n == 10:
                            front_bc(nxt, npar)
                        if n == 11:
                            front_delta(nxt, npar)
                    if back:
                        if n in (5, 6):
                            back_y(prv, ppar, n - 5)
                        if n == 7:
                            back_gate(prv, ppar)
                        if n == 8:
                            back_norm_a(prv, ppar)
                        if n == 9:
                            back_norm_b(prv)
                        if n == 11:
                            back_norm_c(prv)
                        if n == 13:
                            back_norm_d(prv)
                        if n == 15:
                            back_amax(prv)

            front_stats(Pair(0))
            nc.vector.memset(xin[:, :, :, 0:TAPS - 1], 0.0).then_inc(zeroed, 1)
            nc.vector.memset(decay[:, :, :, :, :, 0:1], 0.0).then_inc(zeroed, 1)
            front_norm(Pair(0))
            dve.wait_ge(a_exp_ready, 1)
            nc.vector.tensor_scalar(a_neg[:, :, :], a_exp[:, :, :], -1.0, None, ALU.mult).then_inc(a_neg_ready, 1)
            for h in range(HALVES):
                front_conv(Pair(0), h)
                front_z(Pair(0), h)
            for m in range(HALVES):
                front_dt(Pair(0), m)
            front_bc(Pair(0), 0)
            front_delta(Pair(0), 0)

            def fp8_scale(amax, dst, s, k):
                nc.vector.tensor_scalar(dst[:, 0:1], amax[:, :], 1e-12, None, ALU.max).then_inc(s, 1)
                dve.wait_ge(s, k + 1)
                nc.vector.reciprocal(dst[:, 2:3], dst[:, 0:1]).then_inc(s, 1)
                dve.wait_ge(s, k + 2)
                nc.vector.tensor_scalar(dst[:, 1:2], dst[:, 2:3], FP8_MAX, None, ALU.mult).then_inc(s, 1)
                dve.wait_ge(s, k + 3)

            dve.wait_ge(wq_full, 1)
            nc.vector.tensor_copy(w_ffnT[:, :], bbank[:, 0:P]).then_inc(wq_T, 1)
            dve.wait_ge(wq_T, 1)
            nc.vector.tensor_reduce(wq_amax[:, :], w_ffnT[:, :], AX_X, ALU.max, apply_absolute_value=True)\
                .then_inc(wq_local, 1)
            dve.wait_ge(wq_global, 1)
            fp8_scale(wq_all, wq_scale, wq_step, 0)
            t, m, r = wq_m[:, 0, :], wq_m[:, 1, :], wq_m[:, 2, :]
            nc.vector.tensor_scalar(t, w_ffnT[:, :], wq_scale[:, 1:2], None, ALU.mult).then_inc(wq_step, 1)
            dve.wait_ge(wq_step, 4)
            nc.vector.tensor_scalar(m.bitcast(I32), t.bitcast(I32), EXP_BITS, None, ALU.bitwise_and).then_inc(wq_step, 1)
            dve.wait_ge(wq_step, 5)
            nc.vector.tensor_scalar(m, m, FP8_LEAST, ROUND_AT, ALU.max, ALU.mult).then_inc(wq_step, 1)
            dve.wait_ge(wq_step, 6)
            nc.vector.tensor_tensor(r, t, m, ALU.add).then_inc(wq_step, 1)
            dve.wait_ge(wq_step, 7)
            nc.vector.tensor_tensor(wqT[:, :], r, m, ALU.subtract).then_inc(wq_step, 1)

            slot(Pair(0), 0, True, False)
            with dve.Fori(0, (PAIRS - 2) // 2) as i:
                for k in range(2):
                    slot(Pair(i * 2 + (1 + k), 1 + k), 1 - k, True, True)
            slot(Pair(PAIRS - 1), 1, False, True)
            last_pair = Pair(PAIRS - 1)
            for h in range(HALVES):
                back_y(last_pair, 1, h)
            back_gate(last_pair, 1)
            back_norm_a(last_pair, 1)
            back_norm_b(last_pair)
            back_norm_c(last_pair)
            back_norm_d(last_pair)
            back_amax(last_pair)

            dve.wait_ge(amax_ready, PAIRS)
            nc.vector.tensor_reduce(amax_1[:, :], amax_p[:, :], AX_X, ALU.max).then_inc(x_local, 1)
            dve.wait_ge(x_global, 1)
            fp8_scale(x_amax, x_scale, xs_step, 0)
            nc.vector.tensor_scalar(x_scale[:, 3:4], x_scale[:, 0:1], wq_scale[:, 0:1], 1.0 / FP8_MAX ** 2,
                                    ALU.mult, ALU.mult).then_inc(xs_step, 1)
            dve.wait_ge(xs_step, 4)

            def round_at(grp, par):
                dve.wait_ge(t_ready, nth(grp, 1, 1))
                nc.vector.tensor_scalar(mq[:, par, :].bitcast(I32), tq[:, par, :].bitcast(I32), EXP_BITS, None,
                                        ALU.bitwise_and).then_inc(m_step, 1)
                dve.wait_ge(m_step, nth(grp, 2, 1))
                nc.vector.tensor_scalar(mq[:, par, :], mq[:, par, :], FP8_LEAST, ROUND_AT, ALU.max, ALU.mult)\
                    .then_inc(m_step, 1)

            def rounded(grp, par):
                dve.wait_ge(r_ready, nth(grp, 1, 1))
                if grp.after(2):
                    dve.wait_ge(f_full, grp.v - 1)
                nc.vector.tensor_tensor(xq[:, par, :], rq[:, par, :], mq[:, par, :], ALU.subtract).then_inc(xq_ready, 1)

            def last_stats(grp, par):
                dve.wait_ge(f_full, nth(grp, 1, 1))
                if grp.after(2):
                    dve.wait_ge(f_norm, grp.v - 1)
                nc.vector.scalar_tensor_tensor(out=chunks(ff[:, par, :]), in0=chunks(drive[:, par, 0, :]),
                                               scalar=x_scale[:, 3:4], in1=on_chunks(fb_r[:, :]),
                                               op0=ALU.mult, op1=ALU.add).then_inc(f_ready, 1)
                dve.wait_ge(f_ready, nth(grp, 1, 1))
                for j in range(CH):
                    last = nc.vector.bn_stats(fst[:, j, :], ff[:, par, DM * j:DM * j + DM])
                last.then_inc(f_stats, 1)
                dve.wait_ge(f_stats, nth(grp, 1, 1))
                dve.sem_inc(dve_waited, 1)
                for j in range(CH):
                    last = nc.vector.bn_aggr(fmv[:, j, :], fst[:, j, :])
                last.then_inc(f_mv, 1)
                dve.wait_ge(f_mv, nth(grp, 1, 1))
                nc.vector.tensor_scalar(fvar[:, :], fmv[:, :, 1], LN_EPS, None, ALU.add).then_inc(f_var, 1)

            def shift(grp, par):
                dve.wait_ge(f_rstd, nth(grp, 1, 1))
                nc.vector.scalar_tensor_tensor(out=fshift[:, par, :], in0=fmv[:, :, 0], scalar=-1.0,
                                               in1=frstd[:, par, :], op0=ALU.mult, op1=ALU.mult).then_inc(f_shift, 1)

            def tail(grp, par, new=True, old=True):
                if new:
                    round_at(grp, par)
                if old:
                    last_stats(grp.plus(-1), 1 - par)
                if new:
                    rounded(grp, par)
                if old:
                    shift(grp.plus(-1), 1 - par)

            tail(Pair(0), 0, old=False)
            tail(Pair(1), 1)
            tail(Pair(2), 0)
            with dve.Fori(1, PAIRS // 2 - 1) as i:
                for k in range(2):
                    tail(Pair(i * 2 + (1 + k), 3 + k), 1 - k)
            tail(Pair(PAIRS - 1), 1)
            tail(Pair(PAIRS), 0, new=False)


_INS = ['L0_attn_x', 'L0_attn_W_in', 'L0_attn_b_in', 'L0_attn_conv_w', 'L0_attn_conv_b', 'L0_attn_W_xp',
        'L0_attn_b_xp', 'L0_attn_W_dt', 'L0_attn_b_dt', 'L0_attn_A_log', 'L0_attn_D_skip', 'L0_attn_W_out',
        'L0_attn_b_out', 'L0_attn_alpha', 'L0_attn_beta', 'L0_ffn_weight', 'L0_ffn_bias']
_OUTS = [((BATCH, L, DM), 'float32')]


def kernel(**inputs):
    import numpy as _np
    import concourse.bacc as _bacc
    from concourse import mybir as _mybir
    from concourse.bass_utils import run_bass_kernel_spmd as _run

    nc = _bacc.Bacc("TRN2", target_bir_lowering=False, num_devices=1)
    arrays, args = {}, []
    for name in _INS:
        a = _np.ascontiguousarray(inputs[name])
        arrays[f"in_{name}_dram"] = a
        args.append(nc.dram_tensor(f"in_{name}_dram", a.shape, _mybir.dt.from_np(a.dtype), kind="ExternalInput").ap())
    for i, (shape, dtype) in enumerate(_OUTS):
        dt = _mybir.dt.from_np(_np.dtype(dtype))
        args.append(nc.dram_tensor(f"out_{i}_dram", shape, dt, kind="ExternalOutput").ap())
    build_sandwich(nc, *args)
    r = _run(nc, [arrays], core_ids=[0])
    return r.results[0]["out_0_dram"]
```

```python
from contextlib import ExitStack

import concourse.bass as bass
from concourse import mybir

F32 = mybir.dt.float32
BF16 = mybir.dt.bfloat16
I32 = mybir.dt.int32
ALU = mybir.AluOpType
ACT = mybir.ActivationFunctionType
AX_X = mybir.AxisListType.X
ABSMAX = bass.bass_isa.ReduceOp.absmax

P = 128
DM = 128
DI = 256
HALVES = DI // P
DS = 16
TAPS = 4
L = 256
BATCH = 16
PAIR = 2
PAIRS = BATCH // PAIR
TC = L // P
CH = PAIR * TC
TOK = PAIR * L
SG = 2
UNITS = (DS // SG) * PAIR
BANK = 512

LAG_T, LAG_C, LAG_A = 2, 3, 3
LEAD = 1
DECAYS, DIAGS, STATES, TERMS = 2, 4, 4, 4
SUMS = UNITS - PAIR

LN_EPS = 1e-5
STD_EPS = 1e-6
FP8_MAX = 448.0
EXP_BITS = 0x7F800000
FP8_LEAST = 2.0 ** -6
ROUND_AT = 1.5 * 2.0 ** 20


class Pair:

    def __init__(self, value, least=None):
        self.v = value
        self.least = value if least is None else least

    def plus(self, k):
        return Pair(self.v + k, self.least + k)

    def after(self, d):
        if isinstance(self.v, int):
            return self.v >= d
        assert self.least >= d
        return True


def nth(pair, per, k):
    return pair.v * per + k


def trailing(pair, par, n, lag):
    if n >= lag:
        return pair, par, n - lag
    if not pair.after(1):
        return None
    return pair.plus(-1), 1 - par, n - lag + UNITS


def build_sandwich(nc, x, W_in, b_in, conv_w, conv_b, W_xp, b_xp, W_dt, b_dt, A_log, D_skip,
                   W_out, b_out, alpha, beta, ffn_w, ffn_b, out):
    ctx = ExitStack()
    with ctx:
        def sb(name, shape, dt=F32):
            return ctx.enter_context(nc.sbuf_tensor(name, shape, dt))

        def ps(name, shape):
            return ctx.enter_context(nc.psum_tensor(name, shape, F32))

        def sem(name):
            return ctx.enter_context(nc.semaphore(name))

        x_all = sb("x_all", [P, (PAIRS + 1) * CH * DM])
        h2T = sb("h2T", [DM, PAIRS * TOK])
        w_in = sb("w_in", [P, 2 * DI])
        w_dt = sb("w_dt", [P, HALVES, DI])
        w_xp = sb("w_xp", [P, HALVES, 2 * DS])
        w_out = sb("w_out", [P, HALVES, DM])
        w_ffn = sb("w_ffn", [P, DM])
        w_ffnT = sb("w_ffnT", [P, DM])
        bin_c = sb("bin_c", [P, 2 * HALVES])
        cw = sb("cw", [P, HALVES, TAPS])
        cb = sb("cb", [P, HALVES])
        bdt = sb("bdt", [P, HALVES])
        dskip = sb("dskip", [P, HALVES])
        a_log = sb("a_log", [P, HALVES, DS])
        a_exp = sb("a_exp", [P, HALVES, DS])
        a_neg = sb("a_neg", [P, HALVES, DS])
        bxp_r = sb("bxp_r", [P, 2 * DS])
        bout_r = sb("bout_r", [P, DM])
        alpha_r = sb("alpha_r", [P, DM])
        beta_r = sb("beta_r", [P, DM])
        fb_r = sb("fb_r", [P, DM])
        ident = sb("ident", [P, P])
        minus_half = sb("minus_half", [P, CH])
        half = sb("half", [P, CH])

        st = sb("st", [P, CH, 6])
        mv = sb("mv", [P, CH, 2])
        var1 = sb("var1", [P, CH])
        rstd1 = sb("rstd1", [P, CH])
        xn = sb("xn", [P, 2, CH * DM])
        xnb = sb("xnb", [P, 2, CH * DM])
        xnT = sb("xnT", [DM, TOK])
        xin = sb("xin", [P, HALVES, PAIR, TAPS - 1 + L])
        cv = sb("cv", [P, HALVES, PAIR, L])
        zv = sb("zv", [P, HALVES, TOK])
        xc = sb("xc", [P, 2, HALVES, TOK])
        sz = sb("sz", [P, 2, HALVES, TOK])
        dt_v = sb("dt_v", [P, HALVES, TOK])
        dt_e = sb("dt_e", [P, HALVES, TOK])
        delta = sb("delta", [P, 2, HALVES, PAIR, L])
        u = sb("u", [P, HALVES, TOK])
        uT = sb("uT", [P, 2, CH, DI])
        Bt = sb("Bt", [P, 2, DS // SG, PAIR, TC, SG])
        Ct = sb("Ct", [P, 2, CH, DS])

        decay = sb("decay", [P, DECAYS, HALVES, PAIR, SG, L])
        diag = sb("diag", [P, DIAGS, TC, SG, P])
        state = sb("state", [P, STATES, HALVES, SG, L])
        term = sb("term", [P, TERMS, TC, SG, DI])
        acc = sb("acc", [P, 2, PAIR, TC, SG, DI])
        ysumT = sb("ysumT", [P, CH, DI])

        yv = sb("yv", [P, HALVES, TOK])
        yg = sb("yg", [P, HALVES, TOK])
        res = sb("res", [P, CH * DM])
        nrm = sb("nrm", [P, CH * DM])
        bst = sb("bst", [P, CH, 6])
        bmv = sb("bmv", [P, CH, 2])
        bvar = sb("bvar", [P, CH])
        bstd = sb("bstd", [P, CH])
        bstd2 = sb("bstd2", [P, CH])
        bscale = sb("bscale", [P, CH])
        h2 = sb("h2", [P, CH * DM])
        amax_p = sb("amax_p", [P, PAIRS])
        amax_1 = sb("amax_1", [P, 1])

        wq_amax = sb("wq_amax", [P, 1])
        wq_all = sb("wq_all", [P, 1])
        wq_scale = sb("wq_scale", [P, 4])
        wq_m = sb("wq_m", [P, 3, DM])
        wqT = sb("wqT", [P, DM], BF16)
        x_amax = sb("x_amax", [P, 1])
        x_scale = sb("x_scale", [P, 4])
        xq = sb("xq", [P, 2, TOK], BF16)
        fst = sb("fst", [P, CH, 6])
        fmv = sb("fmv", [P, CH, 2])
        fvar = sb("fvar", [P, CH])
        frstd = sb("frstd", [P, 2, CH])
        fshift = sb("fshift", [P, 2, CH])
        state_flat = state[:, :, :, :, :].rearrange("p r h s t -> p (r h s t)")
        term_flat = term[:, :, :, :, :].rearrange("p r c s t -> p (r c s t)")
        tq, mq, rq, fo = (state_flat[:, 2 * TOK * k:2 * TOK * (k + 1)].rearrange("p (r n) -> p r n", r=2)
                          for k in range(4))
        ff, fn = (term_flat[:, 2 * TOK * k:2 * TOK * (k + 1)].rearrange("p (r n) -> p r n", r=2)
                  for k in range(2))

        drive = ps("drive", [P, 2, HALVES, SG * L])
        hT = ps("hT", [P, TC, SG * DI])
        fbank = ps("fbank", [P, BANK])
        bbank = ps("bbank", [P, BANK])

        dve_waited = sem("dve_waited")
        pool_waited = sem("pool_waited")
        x_first = sem("x_first")
        x_rest = sem("x_rest")
        w_in_loaded = sem("w_in_loaded")
        conv_loaded = sem("conv_loaded")
        wm_loaded = sem("wm_loaded")
        wr_loaded = sem("wr_loaded")
        zeroed = sem("zeroed")
        ident_zero = sem("ident_zero")
        ident_ready = sem("ident_ready")
        consts_ready = sem("consts_ready")
        a_exp_ready = sem("a_exp_ready")
        a_neg_ready = sem("a_neg_ready")
        ln1_stats = sem("ln1_stats")
        ln1_mv = sem("ln1_mv")
        ln1_var = sem("ln1_var")
        ln1_rstd = sem("ln1_rstd")
        xn_ready = sem("xn_ready")
        xnb_ready = sem("xnb_ready")
        xnT_ready = sem("xnT_ready")
        xnT_full = sem("xnT_full")
        front_full = sem("front_full")
        xin_ready = sem("xin_ready")
        conv_tap = sem("conv_tap")
        z_ready = sem("z_ready")
        xc_ready = sem("xc_ready")
        sz_ready = sem("sz_ready")
        dt_ready = sem("dt_ready")
        dt_neg = sem("dt_neg")
        sp_exp = sem("sp_exp")
        sp_log = sem("sp_log")
        delta_ready = sem("delta_ready")
        u_ready = sem("u_ready")
        bc_ready = sem("bc_ready")
        uT_ready = sem("uT_ready")
        decay_ready = sem("decay_ready")
        diag_ready = sem("diag_ready")
        drive_ready = sem("drive_ready")
        scan_done = sem("scan_done")
        hT_ready = sem("hT_ready")
        term_ready = sem("term_ready")
        sum_done = sem("sum_done")
        ysum_ready = sem("ysum_ready")
        back_full = sem("back_full")
        y_ready = sem("y_ready")
        gated = sem("gated")
        res_ready = sem("res_ready")
        b_step = sem("b_step")
        b_var = sem("b_var")
        b_root = sem("b_root")
        h2_ready = sem("h2_ready")
        h2T_ready = sem("h2T_ready")
        amax_ready = sem("amax_ready")
        wq_step = sem("wq_step")
        wq_full = sem("wq_full")
        wq_T = sem("wq_T")
        wq_local = sem("wq_local")
        wq_global = sem("wq_global")
        x_local = sem("x_local")
        x_global = sem("x_global")
        xs_step = sem("xs_step")
        t_ready = sem("t_ready")
        m_step = sem("m_step")
        r_ready = sem("r_ready")
        xq_ready = sem("xq_ready")
        f_full = sem("f_full")
        f_ready = sem("f_ready")
        f_stats = sem("f_stats")
        f_mv = sem("f_mv")
        f_var = sem("f_var")
        f_rstd = sem("f_rstd")
        f_shift = sem("f_shift")
        f_norm = sem("f_norm")
        f_out = sem("f_out")
        stored = [sem("stored_even"), sem("stored_odd")]

        x_v = x.rearrange("b l d -> (b l) d").rearrange("(k p) d -> p k d", p=P)
        out_v = out.rearrange("b l d -> (b l) d").rearrange("(k p) d -> p k d", p=P)
        x_k = x_all[:, :].rearrange("p (k d) -> p k d", d=DM)
        B_STEPS = 13
        block = ctx.enter_context(nc.Block())

        def chunks(t):
            return t.rearrange("p (j d) -> p j d", d=DM)

        def on_chunks(row):
            return row.unsqueeze(1).to_broadcast([P, CH, row.shape[-1]])

        def column(vector):
            return vector.rearrange("(h p) -> p h", p=P)

        def row(vector):
            return vector.rearrange("(a n) -> a n", a=1).to_broadcast([P, vector.shape[0]])

        @block.sync
        def _(sp):
            slow = dict(allow_slow_non_contiguous=True)
            sp.dma_start(x_k[:, 0:CH, :], x_v[:, 0:CH, :]).then_inc(x_first, 16)
            sp.dma_start(w_in[:, :], W_in).then_inc(w_in_loaded, 16)
            sp.dma_start(bin_c[:, :], column(b_in), **slow).then_inc(w_in_loaded, 16)
            sp.dma_start(cw[:, :, :], conv_w.rearrange("(h p) a k -> p h (a k)", p=P)).then_inc(conv_loaded, 16)
            sp.dma_start(cb[:, :], column(conv_b), **slow).then_inc(conv_loaded, 16)
            sp.dma_start(w_dt[:, :, :], W_dt.rearrange("(h p) n -> p h n", p=P)).then_inc(wm_loaded, 16)
            sp.dma_start(bdt[:, :], column(b_dt), **slow).then_inc(wm_loaded, 16)
            sp.dma_start(w_xp[:, :, :], W_xp.rearrange("(h p) n -> p h n", p=P)).then_inc(wm_loaded, 16)
            sp.dma_start(bxp_r[:, :], row(b_xp)).then_inc(wm_loaded, 16)
            sp.dma_start(a_log[:, :, :], A_log.rearrange("(h p) n -> p h n", p=P)).then_inc(wm_loaded, 16)
            sp.dma_start(x_k[:, CH:PAIRS * CH, :], x_v[:, CH:, :]).then_inc(x_rest, 16)
            sp.dma_start(dskip[:, :], column(D_skip), **slow).then_inc(wr_loaded, 16)
            sp.dma_start(w_out[:, :, :], W_out.rearrange("(h p) n -> p h n", p=P)).then_inc(wr_loaded, 16)
            sp.dma_start(bout_r[:, :], row(b_out)).then_inc(wr_loaded, 16)
            sp.dma_start(alpha_r[:, :], row(alpha)).then_inc(wr_loaded, 16)
            sp.dma_start(beta_r[:, :], row(beta)).then_inc(wr_loaded, 16)
            sp.dma_start(fb_r[:, :], row(ffn_b)).then_inc(wr_loaded, 16)
            sp.dma_start(w_ffn[:, :], ffn_w).then_inc(wr_loaded, 16)
            with sp.Fori(0, PAIRS // 2) as i:
                for par in range(2):
                    grp = Pair(i * 2 + par, par)
                    sp.wait_ge(f_out, nth(grp, 1, 1))
                    sp.dma_start(out_v[:, bass.ds(grp.v * CH, CH), :], chunks(fo[:, par, :])).then_inc(stored[par], 16)
            for par in range(2):
                sp.wait_ge(stored[par], 16 * PAIRS // 2)

        @block.gpsimd
        def _(pool):
            pool.memset(ident[:, :], 0.0).then_inc(ident_zero, 1)
            pool.memset(minus_half[:, :], -0.5).then_inc(consts_ready, 1)
            pool.memset(half[:, :], 0.5).then_inc(consts_ready, 1)
            pool.memset(x_all[:, PAIRS * TOK:], 0.0).then_inc(consts_ready, 1)
            pool.wait_ge(ident_zero, 1)
            pool.affine_select(out=ident[:, :], in_=ident[:, :], compare_op=ALU.not_equal, fill=1.0, base=0,
                               pattern=[[-1, P]], channel_multiplier=1).then_inc(ident_ready, 1)
            pool.wait_ge(consts_ready, 3)

            def front_root(pr):
                pool.wait_ge(ln1_var, nth(pr, 1, 1))
                nc.gpsimd.tensor_tensor(rstd1[:, :], var1[:, :], minus_half[:, :], ALU.pow).then_inc(ln1_rstd, 1)

            def front_residual(pr, par):
                pool.wait_ge(xn_ready, nth(pr, 1, 1))
                if pr.after(2):
                    pool.wait_ge(res_ready, nth(pr.plus(-1), 1, 0))
                if not pr.after(1):
                    pool.wait_ge(wr_loaded, 16 * 7)
                nc.gpsimd.tensor_tensor(chunks(xnb[:, par, :]), chunks(xn[:, par, :]), on_chunks(bout_r[:, :]), ALU.add)\
                    .then_inc(xnb_ready, 1)

            def diag_b(pr, par, n):
                g, b = n // PAIR, n % PAIR
                if n == 0:
                    pool.wait_ge(bc_ready, nth(pr, 3, 2))
                old = trailing(pr, par, n, DIAGS)
                if old:
                    pool.wait_ge(drive_ready, nth(old[0], 2 * UNITS, 2 * old[2] + 2))
                pool.sem_inc(pool_waited, 1)
                b_cols = Bt[:, par, g, b, :, :].rearrange("p c s -> p (c s)").unsqueeze(2).to_broadcast([P, TC * SG, P])
                nc.gpsimd.affine_select(out=diag[:, n % DIAGS, :, :, :].rearrange("p c s t -> p (c s) t"), in_=b_cols,
                                        compare_op=ALU.is_equal, fill=0.0, base=0, pattern=[[0, TC * SG], [-1, P]],
                                        channel_multiplier=1).then_inc(diag_ready, 1)

            def add_terms(pr, par, n):
                g, b = n // PAIR, n % PAIR
                if g == 0:
                    return
                pool.wait_ge(term_ready, nth(pr, 2 * UNITS, 2 * n + 2))
                if g > 1:
                    pool.wait_ge(sum_done, nth(pr, SUMS, n - 2 * PAIR + 1))
                a = acc[:, par, b, :, :, :]
                nc.gpsimd.tensor_tensor(a, a, term[:, n % TERMS, :, :, :], ALU.add).then_inc(sum_done, 1)

            def sum_states(pr, par):
                pool.wait_ge(sum_done, nth(pr, SUMS, SUMS))
                for b in range(PAIR):
                    nc.gpsimd.tensor_tensor(ysumT[:, TC * b:TC * b + TC, :], acc[:, par, b, :, 0, :],
                                            acc[:, par, b, :, 1, :], ALU.add).then_inc(ysum_ready, 1)

            def back_root(pr, k):
                pool.wait_ge(b_var, nth(pr, 3, k + 1))
                nc.gpsimd.tensor_tensor(bstd[:, :], bvar[:, :], (half if k == 0 else minus_half)[:, :], ALU.pow)\
                    .then_inc(b_root, 1)

            def slot(pr, par, front, back, units=UNITS):
                for n in range(units):
                    if units == UNITS and n + LEAD < units:
                        diag_b(pr, par, n + LEAD)
                    elif front:
                        diag_b(pr.plus(1), 1 - par, n + LEAD - units)
                    old = trailing(pr, par, n, LAG_A)
                    if old:
                        add_terms(*old)
                    nxt, npar, prv, ppar = pr.plus(1), 1 - par, pr.plus(-1), 1 - par
                    if front:
                        if n == 3:
                            front_root(pr.plus(2))
                        if n == 12:
                            front_residual(nxt, npar)
                    if back:
                        if n == 4:
                            sum_states(prv, ppar)
                        if n in (10, 12, 14):
                            back_root(prv, (n - 10) // 2)

            front_root(Pair(0))
            front_residual(Pair(0), 0)
            front_root(Pair(1))
            pool.wait_ge(wq_local, 1)
            nc.gpsimd.partition_all_reduce(wq_all[:, :], wq_amax[:, :], P, ABSMAX).then_inc(wq_global, 1)
            for n in range(LEAD):
                diag_b(Pair(0), 0, n)
            slot(Pair(0), 0, True, False)
            with pool.Fori(0, (PAIRS - 2) // 2) as i:
                for k in range(2):
                    slot(Pair(i * 2 + (1 + k), 1 + k), 1 - k, True, True)
            slot(Pair(PAIRS - 1), 1, False, True)
            slot(Pair(PAIRS), 0, False, False, LAG_A)
            sum_states(Pair(PAIRS - 1), 1)
            for k in range(3):
                back_root(Pair(PAIRS - 1), k)

            pool.wait_ge(x_local, 1)
            nc.gpsimd.partition_all_reduce(x_amax[:, :], amax_1[:, :], P, ABSMAX).then_inc(x_global, 1)

            def round_up(grp, par):
                pool.wait_ge(t_ready, nth(grp, 1, 1))
                pool.wait_ge(m_step, nth(grp, 2, 2))
                nc.gpsimd.tensor_tensor(rq[:, par, :], tq[:, par, :], mq[:, par, :], ALU.add).then_inc(r_ready, 1)

            def last_root(grp, par):
                pool.wait_ge(f_var, nth(grp, 1, 1))
                nc.gpsimd.tensor_tensor(frstd[:, par, :], fvar[:, :], minus_half[:, :], ALU.pow).then_inc(f_rstd, 1)

            def last_sum(grp, par):
                pool.wait_ge(f_norm, nth(grp, 1, 1))
                if grp.after(2):
                    pool.wait_ge(stored[par], (grp.v - par) * 8)
                nc.gpsimd.tensor_tensor(fo[:, par, :], fn[:, par, :], x_all[:, bass.ds(grp.v * TOK, TOK)], ALU.add)\
                    .then_inc(f_out, 1)

            def tail(grp, par, new=True, old=True):
                if new:
                    round_up(grp, par)
                if old:
                    last_root(grp.plus(-1), 1 - par)
                    last_sum(grp.plus(-1), 1 - par)

            tail(Pair(0), 0, old=False)
            tail(Pair(1), 1)
            tail(Pair(2), 0)
            with pool.Fori(1, PAIRS // 2 - 1) as i:
                for k in range(2):
                    tail(Pair(i * 2 + (1 + k), 3 + k), 1 - k)
            tail(Pair(PAIRS - 1), 1)
            tail(Pair(PAIRS), 0, new=False)

        @block.scalar
        def _(act):
            def front_xnT(pr):
                act.wait_ge(xnT_full, nth(pr, 1, 1))
                nc.scalar.activation(xnT[:, :], fbank[:, :], ACT.Copy).then_inc(xnT_ready, 1)

            def front_xin(pr, h):
                act.wait_ge(front_full, nth(pr, 9, 1 + h))
                if pr.after(1):
                    act.wait_ge(conv_tap, nth(pr.plus(-1), 2 * TAPS, TAPS * (h + 1)))
                nc.scalar.activation(xin[:, h, :, TAPS - 1:], fbank[:, :].rearrange("p (b t) -> p b t", b=PAIR),
                                     ACT.Identity, bias=bin_c[:, h:h + 1]).then_inc(xin_ready, 1)

            def front_silu_x(pr, par):
                act.wait_ge(conv_tap, nth(pr, 2 * TAPS, 2 * TAPS))
                if pr.after(2):
                    act.wait_ge(y_ready, nth(pr.plus(-2), 2, 2))
                nc.scalar.activation(xc[:, par, :, :], cv[:, :, :, :].rearrange("p h b t -> p h (b t)"), ACT.Silu)\
                    .then_inc(xc_ready, 1)

            def front_silu_z(pr, par):
                act.wait_ge(z_ready, nth(pr, 2, 2))
                if pr.after(2):
                    act.wait_ge(gated, nth(pr.plus(-2), 1, 1))
                nc.scalar.activation(sz[:, par, :, :], zv[:, :, :], ACT.Silu).then_inc(sz_ready, 1)

            def front_softplus(pr):
                act.wait_ge(dt_neg, nth(pr, 1, 1))
                nc.scalar.activation(dt_e[:, :, :], dt_e[:, :, :], ACT.Exp).then_inc(sp_exp, 1)
                act.wait_ge(sp_exp, nth(pr, 1, 1))
                nc.scalar.activation(dt_e[:, :, :], dt_e[:, :, :], ACT.Ln, bias=1.0).then_inc(sp_log, 1)

            def front_uT(pr, par, k):
                act.wait_ge(front_full, nth(pr, 9, 8 + k))
                nc.scalar.activation(uT[:, par, 2 * k:2 * k + 2, :],
                                     (bbank if k else fbank)[:, :].rearrange("p (j d) -> p j d", d=DI), ACT.Copy).then_inc(uT_ready, 1)

            def exp_decay(pr, par, g):
                if g == 0:
                    act.wait_ge(delta_ready, nth(pr, 1, 1))
                old = trailing(pr, par, PAIR * g + 1, PAIR * DECAYS)
                if old:
                    act.wait_ge(scan_done, nth(old[0], 2 * UNITS, 2 * old[2] + 2))
                for h in range(HALVES):
                    for s in range(SG):
                        last = nc.scalar.activation(decay[:, g % DECAYS, h, :, s, 1:], delta[:, par, h, :, 1:],
                                                    ACT.Exp, scale=a_neg[:, h, SG * g + s:SG * g + s + 1])
                last.then_inc(decay_ready, 1)

            def scale_c(pr, par, n):
                g, b = n // PAIR, n % PAIR
                if g > 0:
                    old = trailing(pr, par, n, TERMS)
                    if old and old[2] >= PAIR:
                        act.wait_ge(sum_done, nth(old[0], SUMS, old[2] - PAIR + 1))
                if n == 0:
                    act.wait_ge(bc_ready, nth(pr, 3, 3))
                for c in range(TC):
                    act.wait_ge(hT_ready, nth(pr, 2 * UNITS, 2 * n + c + 1))
                    for s in range(SG):
                        dst = acc[:, par, b, c, s, :] if g == 0 else term[:, n % TERMS, c, s, :]
                        last = nc.scalar.activation(dst, hT[:, c, DI * s:DI * s + DI], ACT.Copy,
                                                    scale=Ct[:, par, TC * b + c, SG * g + s:SG * g + s + 1])
                    last.then_inc(term_ready, 1)

            def slot(pr, par, front, back, units=UNITS):
                for n in range(units):
                    if units == UNITS and n % PAIR == 0:
                        exp_decay(pr, par, n // PAIR)
                    old = trailing(pr, par, n, LAG_C)
                    if old:
                        scale_c(*old)
                    nxt, npar = pr.plus(1), 1 - par
                    if front:
                        if n in (1, 2):
                            front_xin(nxt, n - 1)
                        if n == 6:
                            front_xnT(pr.plus(2))
                            front_silu_x(nxt, npar)
                            front_silu_z(nxt, npar)
                        if n == 11:
                            front_softplus(nxt)
                        if n == 15:
                            for k in range(2):
                                front_uT(nxt, npar, k)

            act.wait_ge(zeroed, 2)
            front_xnT(Pair(0))
            act.wait_ge(w_in_loaded, 16 * 2)
            for h in range(HALVES):
                front_xin(Pair(0), h)
            front_silu_x(Pair(0), 0)
            front_silu_z(Pair(0), 0)
            act.wait_ge(wm_loaded, 16 * 5)
            nc.scalar.activation(a_exp[:, :, :], a_log[:, :, :], ACT.Exp).then_inc(a_exp_ready, 1)
            front_softplus(Pair(0))
            for k in range(2):
                front_uT(Pair(0), 0, k)
            front_xnT(Pair(1))
            act.wait_ge(a_neg_ready, 1)
            
            slot(Pair(0), 0, True, False)
            with act.Fori(0, (PAIRS - 2) // 2) as i:
                for k in range(2):
                    slot(Pair(i * 2 + (1 + k), 1 + k), 1 - k, True, True)
            slot(Pair(PAIRS - 1), 1, False, True)
            slot(Pair(PAIRS), 0, False, False, LAG_C)

            def scale_x(grp, par):
                if grp.after(2):
                    act.wait_ge(r_ready, grp.v - 1)
                nc.scalar.activation(tq[:, par, :], h2T[:, bass.ds(grp.v * TOK, TOK)], ACT.Copy,
                                     scale=x_scale[:, 1:2]).then_inc(t_ready, 1)

            def last_norm(grp, par):
                act.wait_ge(f_shift, nth(grp, 1, 1))
                if grp.after(2):
                    act.wait_ge(f_out, grp.v - 1)
                for j in range(CH):
                    last = nc.scalar.activation(fn[:, par, DM * j:DM * j + DM], ff[:, par, DM * j:DM * j + DM],
                                                ACT.Identity, bias=fshift[:, par, j:j + 1],
                                                scale=frstd[:, par, j:j + 1])
                last.then_inc(f_norm, 1)

            def tail(grp, par, new=True, old=True):
                if new:
                    scale_x(grp, par)
                if old:
                    last_norm(grp.plus(-2), par)

            act.wait_ge(xs_step, 3)
            tail(Pair(0), 0, old=False)
            tail(Pair(1), 1, old=False)
            tail(Pair(2), 0)
            tail(Pair(3), 1)
            with act.Fori(2, PAIRS // 2) as i:
                for k in range(2):
                    tail(Pair(i * 2 + k, 4 + k), k)
            tail(Pair(PAIRS), 0, new=False)
            tail(Pair(PAIRS + 1), 1, new=False)

        @block.tensor
        def _(pe):
            front_read = [(xin_ready, 2, 1), (xin_ready, 2, 2), (z_ready, 2, 1), (z_ready, 2, 2),
                          (dt_ready, 2, 1), (dt_ready, 2, 2), (bc_ready, 3, 3), (uT_ready, 2, 1), (uT_ready, 2, 2)]
            back_read = [(y_ready, 2, 1), (y_ready, 2, 2), (res_ready, 1, 1), (h2T_ready, 1, 1)]

            def bank_free(reads, pr, k):
                if k:
                    signal, per, count = reads[k - 1]
                    pe.wait_ge(signal, nth(pr, per, count))

            def front_transpose(pr, par, free=None):
                pe.wait_ge(xn_ready, nth(pr, 1, 1))
                if free:
                    pe.wait_ge(*free)
                for j in range(CH):
                    last = nc.tensor.transpose(fbank[:, P * j:P * j + P], xn[:, par, DM * j:DM * j + DM], ident[:, :])
                last.then_inc(xnT_full, 1)

            def front_in(pr, k):
                if k == 0:
                    pe.wait_ge(xnT_ready, nth(pr, 1, 1))
                    if pr.after(1):
                        pe.wait_ge(uT_ready, nth(pr, 2, 0))
                bank_free(front_read, pr, k)
                nc.tensor.matmul(fbank[:, :], w_in[:, P * k:P * k + P], xnT[:, :], start=True, stop=True)\
                    .then_inc(front_full, 1)

            def front_dt(pr, par, m):
                if m == 0:
                    pe.wait_ge(xc_ready, nth(pr, 1, 1))
                if m == 0 and pr.after(1):
                    pe.wait_ge(xnT_ready, nth(pr, 1, 2))
                bank_free(front_read, pr, 4 + m)
                for h in range(HALVES):
                    last = nc.tensor.matmul(fbank[:, :], w_dt[:, h, P * m:P * m + P], xc[:, par, h, :],
                                            start=(h == 0), stop=(h == HALVES - 1))
                last.then_inc(front_full, 1)

            def front_bc(pr, par):
                bank_free(front_read, pr, 6)
                for j in range(CH):
                    for h in range(HALVES):
                        last = nc.tensor.matmul(fbank[:, 2 * DS * j:2 * DS * (j + 1)], xc[:, par, h, P * j:P * j + P],
                                                w_xp[:, h, :], start=(h == 0), stop=(h == HALVES - 1))
                last.then_inc(front_full, 1)

            def front_ut(pr, k):
                if k == 0:
                    pe.wait_ge(u_ready, nth(pr, 1, 1))
                if k == 0:
                    bank_free(front_read, pr, 7)
                elif pr.after(2):
                    pe.wait_ge(res_ready, nth(pr.plus(-2), 1, 1))
                dst = bbank if k else fbank
                for jj in range(2):
                    j = 2 * k + jj
                    for h in range(HALVES):
                        last = nc.tensor.transpose(dst[:, DI * jj + P * h:DI * jj + P * h + P],
                                                   u[:, h, P * j:P * j + P], ident[:, :])
                last.then_inc(front_full, 1)

            def drive_unit(pr, par, n):
                b = n % PAIR
                if n == 0:
                    pe.wait_ge(uT_ready, nth(pr, 2, 2))
                pe.wait_ge(diag_ready, nth(pr, UNITS, n + 1))
                old = trailing(pr, par, n, 2)
                for h in range(HALVES):
                    if old:
                        pe.wait_ge(scan_done, nth(old[0], 2 * UNITS, 2 * old[2] + h + 1))
                    dst = drive[:, n % 2, h, :].rearrange("p (s t) -> p s t", s=SG)
                    for c in range(TC):
                        last = nc.tensor.matmul(dst[:, :, P * c:P * c + P], uT[:, par, TC * b + c, P * h:P * h + P],
                                                diag[:, n % DIAGS, c, :, :], start=True, stop=True)
                    last.then_inc(drive_ready, 1)

            def transpose_states(pr, par, n):
                pe.wait_ge(scan_done, nth(pr, 2 * UNITS, 2 * n + 2))
                old = trailing(pr, par, n, 1)
                for c in range(TC):
                    if old:
                        pe.wait_ge(term_ready, nth(old[0], 2 * UNITS, 2 * old[2] + c + 1))
                    for s in range(SG):
                        for h in range(HALVES):
                            last = nc.tensor.transpose(hT[:, c, DI * s + P * h:DI * s + P * h + P],
                                                       state[:, n % STATES, h, s, P * c:P * c + P], ident[:, :])
                    last.then_inc(hT_ready, 1)

            def back_y(pr, h):
                if h == 0:
                    pe.wait_ge(ysum_ready, nth(pr, 2, 2))
                bank_free(back_read, pr, h)
                for j in range(CH):
                    last = nc.tensor.transpose(bbank[:, P * j:P * j + P], ysumT[:, j, P * h:P * h + P], ident[:, :])
                last.then_inc(back_full, 1)

            def back_out(pr):
                pe.wait_ge(gated, nth(pr, 1, 1))
                bank_free(back_read, pr, 2)
                for j in range(CH):
                    for h in range(HALVES):
                        last = nc.tensor.matmul(bbank[:, DM * j:DM * j + DM], yg[:, h, P * j:P * j + P],
                                                w_out[:, h, :], start=(h == 0), stop=(h == HALVES - 1))
                last.then_inc(back_full, 1)

            def back_transpose(pr, uT_next=True):
                pe.wait_ge(h2_ready, nth(pr, 1, 1))
                bank_free(back_read, pr, 3)
                if uT_next:
                    pe.wait_ge(uT_ready, nth(pr.plus(2), 2, 2))
                for j in range(CH):
                    last = nc.tensor.transpose(bbank[:, P * j:P * j + P], h2[:, DM * j:DM * j + DM], ident[:, :])
                last.then_inc(back_full, 1)

            def slot(pr, par, front, back, units=UNITS):
                for n in range(units):
                    if units == UNITS:
                        drive_unit(pr, par, n)
                    old = trailing(pr, par, n, LAG_T)
                    if old:
                        transpose_states(*old)
                    nxt, npar, prv = pr.plus(1), 1 - par, pr.plus(-1)
                    if front:
                        if n < 2 * HALVES:
                            front_in(nxt, n)
                        if n == 5:
                            front_transpose(pr.plus(2), par, (z_ready, nth(nxt, 2, 2)))
                        if n in (6, 8):
                            front_dt(nxt, npar, (n - 6) // 2)
                        if n == 10:
                            front_bc(nxt, npar)
                        if n == 14:
                            for k in range(2):
                                front_ut(nxt, k)
                    if back:
                        if n in (4, 5):
                            back_y(prv, n - 4)
                        if n == 7:
                            back_out(prv)
                        if n == 15:
                            back_transpose(prv, front)

            pe.wait_ge(ident_ready, 1)
            front_transpose(Pair(0), 0)
            pe.wait_ge(w_in_loaded, 16 * 2)
            for k in range(2 * HALVES):
                front_in(Pair(0), k)
            pe.wait_ge(wm_loaded, 16 * 5)
            for m in range(HALVES):
                front_dt(Pair(0), 0, m)
            front_bc(Pair(0), 0)
            for k in range(2):
                front_ut(Pair(0), k)
            front_transpose(Pair(1), 1, (uT_ready, 2))
            pe.wait_ge(wr_loaded, 16 * 7)
            nc.tensor.transpose(bbank[:, 0:P], w_ffn[:, :], ident[:, :]).then_inc(wq_full, 1)
            slot(Pair(0), 0, True, False)
            pe.wait_ge(wq_T, 1)
            with pe.Fori(0, (PAIRS - 2) // 2) as i:
                for k in range(2):
                    slot(Pair(i * 2 + (1 + k), 1 + k), 1 - k, True, True)
            slot(Pair(PAIRS - 1), 1, False, True)
            slot(Pair(PAIRS), 0, False, False, LAG_T)
            last_pair = Pair(PAIRS - 1)
            pe.wait_ge(h2T_ready, PAIRS - 1)
            for h in range(HALVES):
                back_y(last_pair, h)
            back_out(last_pair)
            back_transpose(last_pair, False)

            def tail(grp, par):
                pe.wait_ge(xq_ready, nth(grp, 1, 1))
                if grp.after(2):
                    pe.wait_ge(f_ready, grp.v - 1)
                for j in range(CH):
                    last = nc.tensor.matmul(drive[:, par, 0, DM * j:DM * j + DM], xq[:, par, P * j:P * j + P],
                                            wqT[:, :], start=True, stop=True)
                last.then_inc(f_full, 1)

            tail(Pair(0), 0)
            tail(Pair(1), 1)
            with pe.Fori(1, PAIRS // 2) as i:
                for k in range(2):
                    tail(Pair(i * 2 + k, 2 + k), k)

        @block.vector
        def _(dve):
            def front_stats(pr):
                for j in range(CH):
                    nc.vector.bn_stats(st[:, j, :], x_all[:, bass.ds(pr.v * TOK + DM * j, DM)]).then_inc(ln1_stats, 1)
                dve.wait_ge(ln1_stats, nth(pr, CH, CH))
                dve.sem_inc(dve_waited, 1)
                for j in range(CH):
                    nc.vector.bn_aggr(mv[:, j, :], st[:, j, :]).then_inc(ln1_mv, 1)
                dve.wait_ge(ln1_mv, nth(pr, CH, CH))
                nc.vector.tensor_scalar(var1[:, :], mv[:, :, 1], LN_EPS, None, ALU.add).then_inc(ln1_var, 1)

            def front_norm(pr, par):
                dve.wait_ge(ln1_rstd, nth(pr, 1, 1))
                if pr.after(2):
                    dve.wait_ge(xnb_ready, nth(pr.plus(-1), 1, 0))
                for j in range(CH):
                    last = nc.vector.tensor_scalar(xn[:, par, DM * j:DM * j + DM],
                                                   x_all[:, bass.ds(pr.v * TOK + DM * j, DM)],
                                                   mv[:, j, 0:1], rstd1[:, j:j + 1], ALU.subtract, ALU.mult)
                last.then_inc(xn_ready, 1)

            def front_conv(pr, h):
                dve.wait_ge(xin_ready, nth(pr, 2, h + 1))
                y = cv[:, h, :, :]
                nc.vector.tensor_scalar(y, xin[:, h, :, 0:L], cw[:, h, 0:1], cb[:, h:h + 1], ALU.mult, ALU.add)\
                    .then_inc(conv_tap, 1)
                for k in range(1, TAPS):
                    dve.wait_ge(conv_tap, nth(pr, 2 * TAPS, TAPS * h + k))
                    nc.vector.scalar_tensor_tensor(out=y, in0=xin[:, h, :, k:k + L], scalar=cw[:, h, k:k + 1],
                                                   in1=y, op0=ALU.mult, op1=ALU.add).then_inc(conv_tap, 1)

            def front_z(pr, h):
                dve.wait_ge(front_full, nth(pr, 9, 3 + h))
                nc.vector.tensor_scalar(zv[:, h, :], fbank[:, :], bin_c[:, HALVES + h:HALVES + h + 1], None, ALU.add)\
                    .then_inc(z_ready, 1)

            def front_dt(pr, m):
                dve.wait_ge(front_full, nth(pr, 9, 5 + m))
                nc.vector.tensor_scalar(dt_v[:, m, :], fbank[:, :], bdt[:, m:m + 1], None, ALU.add)\
                    .then_inc(dt_ready, 1)
                if m == HALVES - 1:
                    dve.wait_ge(dt_ready, nth(pr, 2, 2))
                    nc.vector.scalar_tensor_tensor(out=dt_e[:, :, :], in0=dt_v[:, :, :], scalar=-1.0,
                                                   in1=dt_v[:, :, :], op0=ALU.mult, op1=ALU.min).then_inc(dt_neg, 1)

            def front_bc(pr, par):
                dve.wait_ge(front_full, nth(pr, 9, 7))
                bc = fbank[:, 0:CH * 2 * DS].rearrange("p (b c n) -> p b c n", b=PAIR, c=TC)
                bias = bxp_r[:, 0:DS].rearrange("p (g s) -> p g s", s=SG).unsqueeze(1).to_broadcast([P, TC, DS // SG, SG])
                for b in range(PAIR):
                    nc.vector.tensor_tensor(Bt[:, par, :, b, :, :].rearrange("p g c s -> p c g s"),
                                            bc[:, b, :, 0:DS].rearrange("p c (g s) -> p c g s", s=SG), bias, ALU.add)\
                        .then_inc(bc_ready, 1)
                nc.vector.tensor_tensor(Ct[:, par, :, :], bc[:, :, :, DS:].rearrange("p b c n -> p (b c) n"),
                                        on_chunks(bxp_r[:, DS:]), ALU.add).then_inc(bc_ready, 1)

            def front_delta(pr, par):
                dve.wait_ge(sp_log, nth(pr, 1, 1))
                d = delta[:, par, :, :, :].rearrange("p h b t -> p h (b t)")
                nc.vector.scalar_tensor_tensor(out=d, in0=dt_v[:, :, :], scalar=0.0, in1=dt_e[:, :, :],
                                               op0=ALU.max, op1=ALU.add).then_inc(delta_ready, 1)
                dve.wait_ge(delta_ready, nth(pr, 1, 1))
                nc.vector.tensor_tensor(u[:, :, :], d, xc[:, par, :, :], ALU.mult).then_inc(u_ready, 1)

            def scan_unit(pr, par, n):
                g, b = n // PAIR, n % PAIR
                if b == 0:
                    dve.wait_ge(decay_ready, nth(pr, UNITS // PAIR, g + 1))
                old = trailing(pr, par, n, STATES)
                if old:
                    dve.wait_ge(hT_ready, nth(old[0], 2 * UNITS, 2 * old[2] + 2))
                for h in range(HALVES):
                    dve.wait_ge(drive_ready, nth(pr, 2 * UNITS, 2 * n + h + 1))
                    nc.vector.tensor_tensor_scan(state[:, n % STATES, h, :, :].rearrange("p s t -> p (s t)"),
                                                 decay[:, g % DECAYS, h, b, :, :].rearrange("p s t -> p (s t)"),
                                                 drive[:, n % 2, h, :], 0.0, ALU.mult, ALU.add).then_inc(scan_done, 1)

            def back_y(pr, par, h):
                dve.wait_ge(back_full, nth(pr, 4, h + 1))
                nc.vector.scalar_tensor_tensor(out=yv[:, h, :], in0=xc[:, par, h, :], scalar=dskip[:, h:h + 1],
                                               in1=bbank[:, :], op0=ALU.mult, op1=ALU.add).then_inc(y_ready, 1)

            def back_gate(pr, par):
                dve.wait_ge(y_ready, nth(pr, 2, 2))
                nc.vector.tensor_tensor(yg[:, :, :], yv[:, :, :], sz[:, par, :, :], ALU.mult).then_inc(gated, 1)

            def b_wait(pr, k):
                dve.wait_ge(b_step, nth(pr, B_STEPS, k))

            def stats_of(pr, src, k):
                for j in range(CH):
                    last = nc.vector.bn_stats(bst[:, j, :], src(j))
                last.then_inc(b_step, 1)
                b_wait(pr, k + 1)
                dve.sem_inc(dve_waited, 1)
                for j in range(CH):
                    last = nc.vector.bn_aggr(bmv[:, j, :], bst[:, j, :])
                last.then_inc(b_step, 1)
                b_wait(pr, k + 2)

            def normalize(dst, src, rs):
                for j in range(CH):
                    last = nc.vector.tensor_scalar(dst(j), src(j), bmv[:, j, 0:1], rs[:, j:j + 1],
                                                   ALU.subtract, ALU.mult)
                return last

            def part(t):
                return lambda j: t[:, DM * j:DM * j + DM]

            def back_norm_a(pr, par):
                dve.wait_ge(back_full, nth(pr, 4, 3))
                dve.wait_ge(xnb_ready, nth(pr, 1, 1))
                nc.vector.tensor_tensor(res[:, :], bbank[:, :], xnb[:, par, :], ALU.add).then_inc(res_ready, 1)
                dve.wait_ge(res_ready, nth(pr, 1, 1))
                stats_of(pr, part(res), 0)
                nc.vector.tensor_scalar(bvar[:, :], bmv[:, :, 1], DM / (DM - 1.0), None, ALU.mult).then_inc(b_var, 1)

            def back_norm_b(pr):
                dve.wait_ge(b_root, nth(pr, 3, 1))
                nc.vector.tensor_scalar(bstd2[:, :], bstd[:, :], STD_EPS, None, ALU.add).then_inc(b_step, 1)
                b_wait(pr, 3)
                nc.vector.reciprocal(bscale[:, :], bstd2[:, :]).then_inc(b_step, 1)
                b_wait(pr, 4)
                normalize(part(nrm), part(res), bscale).then_inc(b_step, 1)
                b_wait(pr, 5)
                nc.vector.tensor_tensor(chunks(nrm[:, :]), chunks(nrm[:, :]), on_chunks(alpha_r[:, :]), ALU.mult)\
                    .then_inc(b_step, 1)
                b_wait(pr, 6)
                nc.vector.tensor_tensor(chunks(nrm[:, :]), chunks(nrm[:, :]), on_chunks(beta_r[:, :]), ALU.add)\
                    .then_inc(b_step, 1)
                b_wait(pr, 7)
                stats_of(pr, part(nrm), 7)
                nc.vector.tensor_scalar(bvar[:, :], bmv[:, :, 1], LN_EPS, None, ALU.add).then_inc(b_var, 1)

            def back_norm_c(pr):
                dve.wait_ge(b_root, nth(pr, 3, 2))
                normalize(part(nrm), part(nrm), bstd).then_inc(b_step, 1)
                b_wait(pr, 10)
                x1 = x_all[:, bass.ds(pr.v * TOK, TOK)]
                nc.vector.tensor_tensor(x1, x1, nrm[:, :], ALU.add).then_inc(b_step, 1)
                b_wait(pr, 11)
                dve.sem_inc(dve_waited, 1)
                stats_of(pr, lambda j: x_all[:, bass.ds(pr.v * TOK + DM * j, DM)], 11)
                nc.vector.tensor_scalar(bvar[:, :], bmv[:, :, 1], LN_EPS, None, ALU.add).then_inc(b_var, 1)

            def back_norm_d(pr):
                dve.wait_ge(b_root, nth(pr, 3, 3))
                normalize(part(h2), lambda j: x_all[:, bass.ds(pr.v * TOK + DM * j, DM)], bstd).then_inc(h2_ready, 1)

            def back_h2T(pr):
                dve.wait_ge(back_full, nth(pr, 4, 4))
                nc.vector.tensor_reduce(amax_p[:, bass.ds(pr.v, 1)], bbank[:, :], AX_X, ALU.max,
                                        apply_absolute_value=True).then_inc(amax_ready, 1)
                nc.vector.tensor_copy(h2T[:, bass.ds(pr.v * TOK, TOK)], bbank[:, :]).then_inc(h2T_ready, 1)

            def slot(pr, par, front, back):
                for n in range(UNITS):
                    scan_unit(pr, par, n)
                    nxt, npar, prv, ppar = pr.plus(1), 1 - par, pr.plus(-1), 1 - par
                    if front:
                        if n == 0:
                            front_stats(pr.plus(2))
                        if n in (1, 2):
                            front_conv(nxt, n - 1)
                        if n in (2, 3):
                            front_z(nxt, n - 2)
                        if n == 3:
                            front_norm(pr.plus(2), par)
                        if n in (6, 8):
                            front_dt(nxt, (n - 6) // 2)
                        if n == 11:
                            front_bc(nxt, npar)
                        if n == 12:
                            front_delta(nxt, npar)
                    if back:
                        if n in (4, 5):
                            back_y(prv, ppar, n - 4)
                        if n == 5:
                            back_gate(prv, ppar)
                        if n == 7:
                            back_norm_a(prv, ppar)
                        if n == 10:
                            back_norm_b(prv)
                        if n == 12:
                            back_norm_c(prv)
                        if n == 14:
                            back_norm_d(prv)
                        if n == 15:
                            back_h2T(prv)

            dve.wait_ge(x_first, 16)
            front_stats(Pair(0))
            nc.vector.memset(xin[:, :, :, 0:TAPS - 1], 0.0).then_inc(zeroed, 1)
            nc.vector.memset(decay[:, :, :, :, :, 0:1], 0.0).then_inc(zeroed, 1)
            front_norm(Pair(0), 0)
            dve.wait_ge(conv_loaded, 16 * 2)
            for h in range(HALVES):
                front_conv(Pair(0), h)
                front_z(Pair(0), h)
            dve.wait_ge(wm_loaded, 16 * 5)
            for m in range(HALVES):
                front_dt(Pair(0), m)
            dve.wait_ge(a_exp_ready, 1)
            nc.vector.tensor_scalar(a_neg[:, :, :], a_exp[:, :, :], -1.0, None, ALU.mult).then_inc(a_neg_ready, 1)
            front_bc(Pair(0), 0)
            front_delta(Pair(0), 0)
            dve.wait_ge(x_rest, 16)
            front_stats(Pair(1))
            front_norm(Pair(1), 1)
            dve.wait_ge(consts_ready, 3)

            def fp8_scale(amax, dst, s, k):
                nc.vector.tensor_scalar(dst[:, 0:1], amax[:, :], 1e-12, None, ALU.max).then_inc(s, 1)
                dve.wait_ge(s, k + 1)
                nc.vector.reciprocal(dst[:, 2:3], dst[:, 0:1]).then_inc(s, 1)
                dve.wait_ge(s, k + 2)
                nc.vector.tensor_scalar(dst[:, 1:2], dst[:, 2:3], FP8_MAX, None, ALU.mult).then_inc(s, 1)
                dve.wait_ge(s, k + 3)

            dve.wait_ge(wq_full, 1)
            nc.vector.tensor_copy(w_ffnT[:, :], bbank[:, 0:P]).then_inc(wq_T, 1)
            dve.wait_ge(wq_T, 1)
            nc.vector.tensor_reduce(wq_amax[:, :], w_ffnT[:, :], AX_X, ALU.max, apply_absolute_value=True)\
                .then_inc(wq_local, 1)
            dve.wait_ge(wq_global, 1)
            fp8_scale(wq_all, wq_scale, wq_step, 0)
            t, m, r = wq_m[:, 0, :], wq_m[:, 1, :], wq_m[:, 2, :]
            nc.vector.tensor_scalar(t, w_ffnT[:, :], wq_scale[:, 1:2], None, ALU.mult).then_inc(wq_step, 1)
            dve.wait_ge(wq_step, 4)
            nc.vector.tensor_scalar(m.bitcast(I32), t.bitcast(I32), EXP_BITS, None, ALU.bitwise_and).then_inc(wq_step, 1)
            dve.wait_ge(wq_step, 5)
            nc.vector.tensor_scalar(m, m, FP8_LEAST, ROUND_AT, ALU.max, ALU.mult).then_inc(wq_step, 1)
            dve.wait_ge(wq_step, 6)
            nc.vector.tensor_tensor(r, t, m, ALU.add).then_inc(wq_step, 1)
            dve.wait_ge(wq_step, 7)
            nc.vector.tensor_tensor(wqT[:, :], r, m, ALU.subtract).then_inc(wq_step, 1)

            slot(Pair(0), 0, True, False)
            with dve.Fori(0, (PAIRS - 2) // 2) as i:
                for k in range(2):
                    slot(Pair(i * 2 + (1 + k), 1 + k), 1 - k, True, True)
            slot(Pair(PAIRS - 1), 1, False, True)
            last_pair = Pair(PAIRS - 1)
            for h in range(HALVES):
                back_y(last_pair, 1, h)
            back_gate(last_pair, 1)
            back_norm_a(last_pair, 1)
            back_norm_b(last_pair)
            back_norm_c(last_pair)
            back_norm_d(last_pair)
            back_h2T(last_pair)

            dve.wait_ge(amax_ready, PAIRS)
            nc.vector.tensor_reduce(amax_1[:, :], amax_p[:, :], AX_X, ALU.max).then_inc(x_local, 1)
            dve.wait_ge(x_global, 1)
            fp8_scale(x_amax, x_scale, xs_step, 0)
            nc.vector.tensor_scalar(x_scale[:, 3:4], x_scale[:, 0:1], wq_scale[:, 0:1], 1.0 / FP8_MAX ** 2,
                                    ALU.mult, ALU.mult).then_inc(xs_step, 1)
            dve.wait_ge(xs_step, 4)

            def round_at(grp, par):
                dve.wait_ge(t_ready, nth(grp, 1, 1))
                nc.vector.tensor_scalar(mq[:, par, :].bitcast(I32), tq[:, par, :].bitcast(I32), EXP_BITS, None,
                                        ALU.bitwise_and).then_inc(m_step, 1)
                dve.wait_ge(m_step, nth(grp, 2, 1))
                nc.vector.tensor_scalar(mq[:, par, :], mq[:, par, :], FP8_LEAST, ROUND_AT, ALU.max, ALU.mult)\
                    .then_inc(m_step, 1)

            def rounded(grp, par):
                dve.wait_ge(r_ready, nth(grp, 1, 1))
                if grp.after(2):
                    dve.wait_ge(f_full, grp.v - 1)
                nc.vector.tensor_tensor(xq[:, par, :], rq[:, par, :], mq[:, par, :], ALU.subtract).then_inc(xq_ready, 1)

            def last_stats(grp, par):
                dve.wait_ge(f_full, nth(grp, 1, 1))
                if grp.after(2):
                    dve.wait_ge(f_norm, grp.v - 1)
                nc.vector.scalar_tensor_tensor(out=chunks(ff[:, par, :]), in0=chunks(drive[:, par, 0, :]),
                                               scalar=x_scale[:, 3:4], in1=on_chunks(fb_r[:, :]),
                                               op0=ALU.mult, op1=ALU.add).then_inc(f_ready, 1)
                dve.wait_ge(f_ready, nth(grp, 1, 1))
                for j in range(CH):
                    last = nc.vector.bn_stats(fst[:, j, :], ff[:, par, DM * j:DM * j + DM])
                last.then_inc(f_stats, 1)
                dve.wait_ge(f_stats, nth(grp, 1, 1))
                dve.sem_inc(dve_waited, 1)
                for j in range(CH):
                    last = nc.vector.bn_aggr(fmv[:, j, :], fst[:, j, :])
                last.then_inc(f_mv, 1)
                dve.wait_ge(f_mv, nth(grp, 1, 1))
                nc.vector.tensor_scalar(fvar[:, :], fmv[:, :, 1], LN_EPS, None, ALU.add).then_inc(f_var, 1)

            def shift(grp, par):
                dve.wait_ge(f_rstd, nth(grp, 1, 1))
                nc.vector.scalar_tensor_tensor(out=fshift[:, par, :], in0=fmv[:, :, 0], scalar=-1.0,
                                               in1=frstd[:, par, :], op0=ALU.mult, op1=ALU.mult).then_inc(f_shift, 1)

            def tail(grp, par, new=True, old=True):
                if new:
                    round_at(grp, par)
                if old:
                    last_stats(grp.plus(-1), 1 - par)
                if new:
                    rounded(grp, par)
                if old:
                    shift(grp.plus(-1), 1 - par)

            tail(Pair(0), 0, old=False)
            tail(Pair(1), 1)
            tail(Pair(2), 0)
            with dve.Fori(1, PAIRS // 2 - 1) as i:
                for k in range(2):
                    tail(Pair(i * 2 + (1 + k), 3 + k), 1 - k)
            tail(Pair(PAIRS - 1), 1)
            tail(Pair(PAIRS), 0, new=False)


_INS = ['L0_attn_x', 'L0_attn_W_in', 'L0_attn_b_in', 'L0_attn_conv_w', 'L0_attn_conv_b', 'L0_attn_W_xp',
        'L0_attn_b_xp', 'L0_attn_W_dt', 'L0_attn_b_dt', 'L0_attn_A_log', 'L0_attn_D_skip', 'L0_attn_W_out',
        'L0_attn_b_out', 'L0_attn_alpha', 'L0_attn_beta', 'L0_ffn_weight', 'L0_ffn_bias']
_OUTS = [((BATCH, L, DM), 'float32')]


def kernel(**inputs):
    import numpy as _np
    import concourse.bacc as _bacc
    from concourse import mybir as _mybir
    from concourse.bass_utils import run_bass_kernel_spmd as _run

    nc = _bacc.Bacc("TRN2", target_bir_lowering=False, num_devices=1)
    arrays, args = {}, []
    for name in _INS:
        a = _np.ascontiguousarray(inputs[name])
        arrays[f"in_{name}_dram"] = a
        args.append(nc.dram_tensor(f"in_{name}_dram", a.shape, _mybir.dt.from_np(a.dtype), kind="ExternalInput").ap())
    for i, (shape, dtype) in enumerate(_OUTS):
        dt = _mybir.dt.from_np(_np.dtype(dtype))
        args.append(nc.dram_tensor(f"out_{i}_dram", shape, dt, kind="ExternalOutput").ap())
    build_sandwich(nc, *args)
    r = _run(nc, [arrays], core_ids=[0])
    return r.results[0]["out_0_dram"]
```
